# Optimizing a Trainium2 kernel written in Bass

```python
import numpy as np
import jax
import jax.numpy as jnp

def _softmax(x, axis=-1):
    return jax.nn.softmax(x, axis=axis)

def _gelu(x):
    return jax.nn.gelu(x, approximate=True)

def _silu(x):
    return jax.nn.silu(x)

def _sigmoid(x):
    return jax.nn.sigmoid(x)

def _layernorm(x, axis=-1, eps=1e-05):
    m = jnp.mean(x, axis=axis, keepdims=True)
    v = jnp.var(x, axis=axis, keepdims=True)
    return (x - m) / jnp.sqrt(v + eps)

def _scatter_add(tgt, idx, src, axis=0):
    return tgt.at[idx].add(src)

def _segment_sum(src, seg, n):
    return jax.ops.segment_sum(src, seg, n)
kernel_name = 'mk_vit_tower_cls_d1_tok_img768_r4_5011b3'

def setup_inputs(seed: int=0):
    np.random.seed(seed)
    _w = jnp.asarray

    def _rec_inputs():
        import jax
        import jax.numpy as jnp
        _rk = jax.random.key(seed)
        x = -0.000125008 + 0.999885 * jax.random.normal(jax.random.fold_in(_rk, 1), (32, 1, 96, 96), jnp.float32)
        cls_tok = 0.02 * jax.random.normal(jax.random.fold_in(_rk, 5), (1, 1, 192), jnp.float32)
        return (x, cls_tok)
    x, cls_tok = _rec_inputs()

    def _L0_tok_setup():
        import jax, jax.numpy as jnp
        import numpy as np
        PATCH = 16
        LATENT = 192

        def _extract_patches(x, p):
            B, C, H, W_ = x.shape
            nh, nw = (H // p, W_ // p)
            patches = x.reshape(B, C, nh, p, nw, p).transpose(0, 1, 2, 4, 3, 5)
            return patches.reshape(B, nh * nw, C * p * p)
        key = jax.random.key(seed)
        k1, k2 = jax.random.split(key)
        x = jax.random.normal(k1, (32, 1, 256, 256), dtype=jnp.float32)
        W = jax.random.normal(k2, (LATENT, PATCH * PATCH), dtype=jnp.float32) * 0.02
        return {'x': x, 'W': W}
    _L0_tok_all = _L0_tok_setup()
    _L0_tok_in = {k: v for k, v in _L0_tok_all.items() if k in ('W',)}
    del _L0_tok_all

    def _L0_attn_setup():
        import jax, jax.numpy as jnp
        import numpy as np
        EPS = 1e-05
        B, T, C = (8, 512, 192)
        H = 4 * C
        LAYER_ID, N_LAYER = (4, 12)

        def _ln(x, w, b):
            mu = x.mean(-1, keepdims=True)
            var = ((x - mu) ** 2).mean(-1, keepdims=True)
            return (x - mu) / jnp.sqrt(var + EPS) * w + b

        def _wkv_scan(w, k, v):
            a0 = jnp.zeros(k.shape[1:], k.dtype)
            b0 = jnp.zeros_like(a0)
            m0 = jnp.full_like(a0, -1e+38)

            def step(carry, kv):
                a, b, m = carry
                kt, vt = kv
                mm = jnp.maximum(m + w, kt)
                e1 = jnp.exp(m + w - mm)
                e2 = jnp.exp(kt - mm)
                return ((e1 * a + e2 * vt, e1 * b + e2, mm), (a, b, m))
            _, (A, Bd, M) = jax.lax.scan(step, (a0, b0, m0), (k, v))
            return (A, Bd, M)

        def bi_wkv(w, u, k, v):
            kt = jnp.swapaxes(k, 0, 1)
            vt = jnp.swapaxes(v, 0, 1)
            af, bf, mf = _wkv_scan(w, kt, vt)
            ab, bb, mb = _wkv_scan(w, kt[::-1], vt[::-1])
            ab, bb, mb = (ab[::-1], bb[::-1], mb[::-1])
            kk = kt + u
            M = jnp.maximum(jnp.maximum(mf, mb), kk)
            ef = jnp.exp(mf - M)
            eb = jnp.exp(mb - M)
            ec = jnp.exp(kk - M)
            y = (ef * af + eb * ab + ec * vt) / (ef * bf + eb * bb + ec)
            return jnp.swapaxes(y, 0, 1)
        key = jax.random.key(seed)
        ks = jax.random.split(key, 9)
        x = jax.random.normal(ks[0], (B, T, C), jnp.float32)
        r01 = LAYER_ID / (N_LAYER - 1)
        h = np.arange(C, dtype=np.float64)
        decay = (-5.0 + 8.0 * (h / (C - 1)) ** (0.7 + 1.3 * r01)).astype(np.float32)
        zigzag = ((np.arange(C) + 1) % 3 - 1).astype(np.float32) * 0.5
        first = (np.float32(np.log(0.3)) + zigzag).astype(np.float32)
        s = 0.02
        return {'x': x, 'ln1_w': jnp.ones((C,), jnp.float32), 'ln1_b': jnp.zeros((C,), jnp.float32), 'ln2_w': jnp.ones((C,), jnp.float32), 'ln2_b': jnp.zeros((C,), jnp.float32), 'decay': jnp.asarray(decay), 'first': jnp.asarray(first), 'Wk_a': s * jax.random.normal(ks[1], (C, C), jnp.float32), 'Wv_a': s * jax.random.normal(ks[2], (C, C), jnp.float32), 'Wr_a': s * jax.random.normal(ks[3], (C, C), jnp.float32), 'Wo_a': s * jax.random.normal(ks[4], (C, C), jnp.float32), 'Wk_f': s * jax.random.normal(ks[5], (H, C), jnp.float32), 'Wv_f': s * jax.random.normal(ks[6], (C, H), jnp.float32), 'Wr_f': s * jax.random.normal(ks[7], (C, C), jnp.float32)}
    _L0_attn_all = _L0_attn_setup()
    _L0_attn_in = {k: v for k, v in _L0_attn_all.items() if k in ('ln1_w', 'ln1_b', 'ln2_w', 'ln2_b', 'decay', 'first', 'Wk_a', 'Wv_a', 'Wr_a', 'Wo_a', 'Wk_f', 'Wv_f', 'Wr_f')}
    del _L0_attn_all

    def _L0_ffn_setup():
        import jax, jax.numpy as jnp
        import numpy as np
        H = 192
        I = 96
        E = 16
        G = 4
        TOPK_GROUP = 2
        TOP_K = 4
        SCALE = 2.5
        N_SHARED = 2
        IS = I * N_SHARED
        B, S = (1, 512)

        def _route(x, router_w, router_b, corr_bias):
            logits = x.astype(jnp.float32) @ router_w.T + router_b
            scores = jax.nn.sigmoid(logits)
            sfc = scores + corr_bias[None, :]
            grp = sfc.reshape(-1, G, E // G)
            group_scores = jax.lax.top_k(grp, 2)[0].sum(-1)
            _, gidx = jax.lax.top_k(group_scores, TOPK_GROUP)
            gmask = jax.nn.one_hot(gidx, G, dtype=sfc.dtype).sum(axis=1)
            score_mask = jnp.repeat(gmask, E // G, axis=-1)
            sfc = jnp.where(score_mask > 0, sfc, 0.0)
            _, idx = jax.lax.top_k(sfc, TOP_K)
            w = jnp.take_along_axis(scores, idx, axis=1)
            w = w / (w.sum(-1, keepdims=True) + 1e-20)
            return (idx, w * SCALE)

        def _forward(x3, router_w, router_b, corr_bias, gWg, gbg, gWu, gbu, gWd, gbd, sWg, sbg, sWu, sbu, sWd, sbd):
            orig_shape = x3.shape
            x = x3.reshape(-1, H)
            idx, w = _route(x, router_w, router_b, corr_bias)
            c = (jax.nn.one_hot(idx, E, dtype=w.dtype) * w[..., None]).sum(1)
            h = jax.nn.silu(jnp.einsum('th,ehi->tei', x, gWg) + gbg) * (jnp.einsum('th,ehi->tei', x, gWu) + gbu)
            out_e = jnp.einsum('tei,eih->teh', h, gWd) + gbd
            moe_out = jnp.einsum('te,teh->th', c, out_e)
            hs = jax.nn.silu(x @ sWg + sbg) * (x @ sWu + sbu)
            shared = hs @ sWd + sbd
            return (moe_out + shared).reshape(orig_shape)
        key = jax.random.key(seed)
        ks = jax.random.split(key, 16)
        s = lambda k, shape, fan: jax.random.normal(k, shape, jnp.float32) * fan ** (-0.5)
        return {'hidden_states': jax.random.normal(ks[0], (B, S, H), jnp.float32), 'router_w': s(ks[1], (E, H), H), 'router_b': jnp.zeros((E,), jnp.float32), 'corr_bias': jnp.zeros((E,), jnp.float32), 'gWg': s(ks[2], (E, H, I), H), 'gbg': jnp.zeros((E, I), jnp.float32), 'gWu': s(ks[3], (E, H, I), H), 'gbu': jnp.zeros((E, I), jnp.float32), 'gWd': s(ks[4], (E, I, H), I), 'gbd': jnp.zeros((E, H), jnp.float32), 'sWg': s(ks[5], (H, IS), H), 'sbg': jnp.zeros((IS,), jnp.float32), 'sWu': s(ks[6], (H, IS), H), 'sbu': jnp.zeros((IS,), jnp.float32), 'sWd': s(ks[7], (IS, H), IS), 'sbd': jnp.zeros((H,), jnp.float32)}
    _L0_ffn_all = _L0_ffn_setup()
    _L0_ffn_in = {k: v for k, v in _L0_ffn_all.items() if k in ('router_w', 'router_b', 'corr_bias', 'gWg', 'gbg', 'gWu', 'gbu', 'gWd', 'gbd', 'sWg', 'sbg', 'sWu', 'sbu', 'sWd', 'sbd')}
    del _L0_ffn_all
    return {'x': x, 'cls_tok': cls_tok, 'L0_tok_W': _L0_tok_in['W'], 'L0_attn_ln1_w': _L0_attn_in['ln1_w'], 'L0_attn_ln1_b': _L0_attn_in['ln1_b'], 'L0_attn_ln2_w': _L0_attn_in['ln2_w'], 'L0_attn_ln2_b': _L0_attn_in['ln2_b'], 'L0_attn_decay': _L0_attn_in['decay'], 'L0_attn_first': _L0_attn_in['first'], 'L0_attn_Wk_a': _L0_attn_in['Wk_a'], 'L0_attn_Wv_a': _L0_attn_in['Wv_a'], 'L0_attn_Wr_a': _L0_attn_in['Wr_a'], 'L0_attn_Wo_a': _L0_attn_in['Wo_a'], 'L0_attn_Wk_f': _L0_attn_in['Wk_f'], 'L0_attn_Wv_f': _L0_attn_in['Wv_f'], 'L0_attn_Wr_f': _L0_attn_in['Wr_f'], 'L0_ffn_router_w': _L0_ffn_in['router_w'], 'L0_ffn_router_b': _L0_ffn_in['router_b'], 'L0_ffn_corr_bias': _L0_ffn_in['corr_bias'], 'L0_ffn_gWg': _L0_ffn_in['gWg'], 'L0_ffn_gbg': _L0_ffn_in['gbg'], 'L0_ffn_gWu': _L0_ffn_in['gWu'], 'L0_ffn_gbu': _L0_ffn_in['gbu'], 'L0_ffn_gWd': _L0_ffn_in['gWd'], 'L0_ffn_gbd': _L0_ffn_in['gbd'], 'L0_ffn_sWg': _L0_ffn_in['sWg'], 'L0_ffn_sbg': _L0_ffn_in['sbg'], 'L0_ffn_sWu': _L0_ffn_in['sWu'], 'L0_ffn_sbu': _L0_ffn_in['sbu'], 'L0_ffn_sWd': _L0_ffn_in['sWd'], 'L0_ffn_sbd': _L0_ffn_in['sbd']}

def reference(x, cls_tok, L0_tok_W, L0_attn_ln1_w, L0_attn_ln1_b, L0_attn_ln2_w, L0_attn_ln2_b, L0_attn_decay, L0_attn_first, L0_attn_Wk_a, L0_attn_Wv_a, L0_attn_Wr_a, L0_attn_Wo_a, L0_attn_Wk_f, L0_attn_Wv_f, L0_attn_Wr_f, L0_ffn_router_w, L0_ffn_router_b, L0_ffn_corr_bias, L0_ffn_gWg, L0_ffn_gbg, L0_ffn_gWu, L0_ffn_gbu, L0_ffn_gWd, L0_ffn_gbd, L0_ffn_sWg, L0_ffn_sbg, L0_ffn_sWu, L0_ffn_sbu, L0_ffn_sWd, L0_ffn_sbd):
    import jax
    import jax.numpy as jnp

    def _L0_tok_ref(x, W):
        import jax, jax.numpy as jnp
        import numpy as np
        PATCH = 16
        LATENT = 192

        def _extract_patches(x, p):
            B, C, H, W_ = x.shape
            nh, nw = (H // p, W_ // p)
            patches = x.reshape(B, C, nh, p, nw, p).transpose(0, 1, 2, 4, 3, 5)
            return patches.reshape(B, nh * nw, C * p * p)
        patches = _extract_patches(x, PATCH)
        return jnp.einsum('bnk,ok->bno', patches, W)

    def _L0_attn_ref(x, ln1_w, ln1_b, ln2_w, ln2_b, decay, first, Wk_a, Wv_a, Wr_a, Wo_a, Wk_f, Wv_f, Wr_f):
        import jax, jax.numpy as jnp
        import numpy as np
        EPS = 1e-05
        B, T, C = (8, 512, 192)
        H = 4 * C
        LAYER_ID, N_LAYER = (4, 12)

        def _ln(x, w, b):
            mu = x.mean(-1, keepdims=True)
            var = ((x - mu) ** 2).mean(-1, keepdims=True)
            return (x - mu) / jnp.sqrt(var + EPS) * w + b

        def _wkv_scan(w, k, v):
            a0 = jnp.zeros(k.shape[1:], k.dtype)
            b0 = jnp.zeros_like(a0)
            m0 = jnp.full_like(a0, -1e+38)

            def step(carry, kv):
                a, b, m = carry
                kt, vt = kv
                mm = jnp.maximum(m + w, kt)
                e1 = jnp.exp(m + w - mm)
                e2 = jnp.exp(kt - mm)
                return ((e1 * a + e2 * vt, e1 * b + e2, mm), (a, b, m))
            _, (A, Bd, M) = jax.lax.scan(step, (a0, b0, m0), (k, v))
            return (A, Bd, M)

        def bi_wkv(w, u, k, v):
            kt = jnp.swapaxes(k, 0, 1)
            vt = jnp.swapaxes(v, 0, 1)
            af, bf, mf = _wkv_scan(w, kt, vt)
            ab, bb, mb = _wkv_scan(w, kt[::-1], vt[::-1])
            ab, bb, mb = (ab[::-1], bb[::-1], mb[::-1])
            kk = kt + u
            M = jnp.maximum(jnp.maximum(mf, mb), kk)
            ef = jnp.exp(mf - M)
            eb = jnp.exp(mb - M)
            ec = jnp.exp(kk - M)
            y = (ef * af + eb * ab + ec * vt) / (ef * bf + eb * bb + ec)
            return jnp.swapaxes(y, 0, 1)
        Bn, Tn, Cn = x.shape
        h = _ln(x, ln1_w, ln1_b)
        k = h @ Wk_a.T
        v = h @ Wv_a.T
        sr = jax.nn.sigmoid(h @ Wr_a.T)
        y = bi_wkv(decay / Tn, first / Tn, k, v)
        x = x + sr * y @ Wo_a.T
        h = _ln(x, ln2_w, ln2_b)
        kf = jnp.square(jax.nn.relu(h @ Wk_f.T))
        x = x + jax.nn.sigmoid(h @ Wr_f.T) * (kf @ Wv_f.T)
        return x

    def _L0_ffn_ref(hidden_states, router_w, router_b, corr_bias, gWg, gbg, gWu, gbu, gWd, gbd, sWg, sbg, sWu, sbu, sWd, sbd):
        import jax, jax.numpy as jnp
        import numpy as np
        H = 192
        I = 96
        E = 16
        G = 4
        TOPK_GROUP = 2
        TOP_K = 4
        SCALE = 2.5
        N_SHARED = 2
        IS = I * N_SHARED
        B, S = (1, 512)

        def _route(x, router_w, router_b, corr_bias):
            logits = x.astype(jnp.float32) @ router_w.T + router_b
            scores = jax.nn.sigmoid(logits)
            sfc = scores + corr_bias[None, :]
            grp = sfc.reshape(-1, G, E // G)
            group_scores = jax.lax.top_k(grp, 2)[0].sum(-1)
            _, gidx = jax.lax.top_k(group_scores, TOPK_GROUP)
            gmask = jax.nn.one_hot(gidx, G, dtype=sfc.dtype).sum(axis=1)
            score_mask = jnp.repeat(gmask, E // G, axis=-1)
            sfc = jnp.where(score_mask > 0, sfc, 0.0)
            _, idx = jax.lax.top_k(sfc, TOP_K)
            w = jnp.take_along_axis(scores, idx, axis=1)
            w = w / (w.sum(-1, keepdims=True) + 1e-20)
            return (idx, w * SCALE)

        def _forward(x3, router_w, router_b, corr_bias, gWg, gbg, gWu, gbu, gWd, gbd, sWg, sbg, sWu, sbu, sWd, sbd):
            orig_shape = x3.shape
            x = x3.reshape(-1, H)
            idx, w = _route(x, router_w, router_b, corr_bias)
            c = (jax.nn.one_hot(idx, E, dtype=w.dtype) * w[..., None]).sum(1)
            h = jax.nn.silu(jnp.einsum('th,ehi->tei', x, gWg) + gbg) * (jnp.einsum('th,ehi->tei', x, gWu) + gbu)
            out_e = jnp.einsum('tei,eih->teh', h, gWd) + gbd
            moe_out = jnp.einsum('te,teh->th', c, out_e)
            hs = jax.nn.silu(x @ sWg + sbg) * (x @ sWu + sbu)
            shared = hs @ sWd + sbd
            return (moe_out + shared).reshape(orig_shape)
        return _forward(hidden_states, router_w, router_b, corr_bias, gWg, gbg, gWu, gbu, gWd, gbd, sWg, sbg, sWu, sbu, sWd, sbd)
    h = _L0_tok_ref(x, L0_tok_W)
    h = jnp.concatenate([jnp.broadcast_to(cls_tok, (h.shape[0], 1, h.shape[2])), h], axis=1)
    h = h + _L0_attn_ref(_layernorm(h, axis=-1), L0_attn_ln1_w, L0_attn_ln1_b, L0_attn_ln2_w, L0_attn_ln2_b, L0_attn_decay, L0_attn_first, L0_attn_Wk_a, L0_attn_Wv_a, L0_attn_Wr_a, L0_attn_Wo_a, L0_attn_Wk_f, L0_attn_Wv_f, L0_attn_Wr_f)
    h = h + _L0_ffn_ref(_layernorm(h, axis=-1), L0_ffn_router_w, L0_ffn_router_b, L0_ffn_corr_bias, L0_ffn_gWg, L0_ffn_gbg, L0_ffn_gWu, L0_ffn_gbu, L0_ffn_gWd, L0_ffn_gbd, L0_ffn_sWg, L0_ffn_sbg, L0_ffn_sWu, L0_ffn_sbu, L0_ffn_sWd, L0_ffn_sbd)
    return h

_drawn_inputs = setup_inputs


def setup_inputs(seed=0):
    import zlib

    import numpy as np

    out = dict(_drawn_inputs(seed))
    spreads = {'L0_attn_ln1_w': (1.0, 0.6),
     'L0_attn_ln1_b': (0.0, 0.419),
     'L0_attn_ln2_w': (1.0, 0.564),
     'L0_attn_ln2_b': (0.0, 0.694),
     'L0_ffn_router_b': (0.0, 0.1),
     'L0_ffn_corr_bias': (0.0, 0.1),
     'L0_ffn_gbg': (0.0, 0.1),
     'L0_ffn_gbu': (0.0, 0.1),
     'L0_ffn_gbd': (0.0, 0.1),
     'L0_ffn_sbg': (0.0, 0.1),
     'L0_ffn_sbu': (0.0, 0.1),
     'L0_ffn_sbd': (0.0, 0.1)}
    factors = {'L0_attn_decay': 3.737,
     'L0_attn_first': 8.0,
     'L0_attn_Wk_a': 3.129,
     'L0_attn_Wr_a': 5.288,
     'L0_attn_Wr_f': 3.552}
    for name, (base, spread) in spreads.items():
        noise = np.random.default_rng([zlib.crc32(name.encode()), seed]).standard_normal(out[name].shape)
        drawn = base * np.exp(spread * noise) if base else spread * noise
        out[name] = jnp.asarray(drawn.astype(out[name].dtype))
    for name, factor in factors.items():
        out[name] = (out[name] * factor).astype(out[name].dtype)
    return out
```

```python
from contextlib import ExitStack

import concourse.bass as bass
from concourse import mybir

F32, F32R, I32 = mybir.dt.float32, mybir.dt.float32r, mybir.dt.int32
ALU, ACT = mybir.AluOpType, mybir.ActivationFunctionType
AXX = mybir.AxisListType.X

BATCH, SIDE, PATCH, C = 32, 6, 16, 192
T = SIDE * SIDE + 1
PIX = PATCH * PATCH
GROUPS = 4
IMGS = BATCH // GROUPS
N = IMGS * T
TILES = 3
TP = -(-N // TILES // 2) * 2
TS = [0, (N - TP) // 4 * 2, N - TP]
HALF = C // 2
HID = 4 * C
UPS = HID // 128
EXPERTS, INNER, EGROUPS, TOPG, TOPK = 16, 96, 4, 2, 4
EPG = EXPERTS // EGROUPS
ECH = EXPERTS * INNER // 128
SCH = 2
SCALE = 2.5
EPS = 1e-5
NEG = -1e38
CROWS = 3 * EXPERTS
RSQRT_SEED = float(0x5F3759DF)
W2 = 2 * N
SEQS = 2 * IMGS

def _pieces():
    stacked = lambda name, cols: (name, 128, 2, cols, True)
    yield stacked("tok", C)
    yield from (stacked(m, C) for m in ("k", "v", "r"))
    yield ("o", HALF, 2, C, True)
    yield stacked("rf", C)
    yield from (stacked(f"up{i}", HID // 2) for i in range(2))
    yield from ((f"down{i}", 128, UPS // 2, C, True) for i in range(2))
    yield stacked("router", EXPERTS)
    yield stacked("sgu", 2 * C)
    yield ("sd", INNER, SCH, C, True)
    yield ("bd", CROWS, 1, C, False)
    yield from ((f"sel{i}", CROWS, ECH // 2, 128, False) for i in range(2))
    for i in range(ECH // 2):
        yield stacked(f"egu{i}", 512)
        if i % 2 == 0:
            yield (f"ed{i // 2}", 128, 4, C, True)


PIECES = list(_pieces())
PIECE_AT = {p[0]: n for n, p in enumerate(PIECES)}
RING, RING_COLS = 3, 2 * 512


def build(nc, A):
    ctx = ExitStack()
    with ctx:
        def sb(name, shape, dt=F32):
            return ctx.enter_context(nc.sbuf_tensor(name, shape, dt))

        def pb(name, shape):
            return ctx.enter_context(nc.psum_tensor(name, shape, F32))

        def sem(name):
            return ctx.enter_context(nc.semaphore(name))

        per_group = {}

        def counted(name, n):
            s = sem(name)
            per_group[s] = n
            return s

        def at(s, g, n):
            return g * per_group[s] + n

        hi = {p[0]: sb(f"hi_{p[0]}", [p[1], p[2], p[3]], F32R) for p in PIECES}
        lo = {p[0]: sb(f"lo_{p[0]}", [p[1], p[2], p[3]], F32R) for p in PIECES if p[4]}
        raw = [sb(f"raw{i}", [128, RING_COLS]) for i in range(RING)]
        ident32, ident = sb("ident32", [128, 128]), sb("ident", [128, 128], F32R)
        ones_e = sb("ones_e", [TP, EXPERTS])
        cls_rows = sb("cls_rows", [TP, TILES, C])
        ln1w, ln1b = sb("ln1w", [TP, C]), sb("ln1b", [TP, C])
        ln2w, ln2b = sb("ln2w", [TP, C]), sb("ln2b", [TP, C])
        sbd = sb("sbd", [TP, C])
        rbias, cbias = sb("rbias", [TP, EXPERTS]), sb("cbias", [TP, EXPERTS])
        before = sb("before", [TP, EGROUPS, EGROUPS])
        decay, first = sb("decay", [HALF, 2]), sb("first", [HALF, 2])
        dec_f, dec_b = sb("dec_f", [HALF, W2]), sb("dec_b", [HALF, W2])
        egb, eub = sb("egb", [128, ECH]), sb("eub", [128, ECH])
        sgb, sub_ = sb("sgb", [INNER, SCH]), sb("sub_", [INNER, SCH])
        nothing, spare_v = sb("nothing", [128, len(PIECES)]), sb("spare_v", [128, 8])
        pat = sb("pat", [128, 2, N])
        pat_hi, pat_lo = sb("pat_hi", [128, 2, N], F32R), sb("pat_lo", [128, 2, N], F32R)
        h0, x0, norm, h1 = (sb(n, [TP, TILES, C]) for n in ("h0", "x0", "norm", "h1"))
        split = sb("split", [TP, TILES, 2 * C], F32R)
        stats, mv = sb("stats", [TP, TILES, 6]), sb("mv", [TP, TILES, 2])
        var, rstd, ny = (sb(n, [TP, 2, TILES]) for n in ("var", "rstd", "ny"))
        seed = sb("seed", [TP, 2, TILES], I32)
        stack = [sb(f"stack{i}", [128, 3, N], F32R) for i in range(2)]
        stack = [stack[0], stack[0], stack[1]]
        K, V, R = sb("K", [HALF, W2]), sb("V", [HALF, W2]), sb("R", [HALF, W2])
        M = [sb("Mf", [HALF, W2 + 1]), sb("Mb", [HALF, W2 + 1])]
        E1 = [sb("E1f", [HALF, W2]), sb("E1b", [HALF, W2])]
        SB = [sb("SBf", [HALF, W2 + 1]), sb("SBb", [HALF, W2 + 1])]
        SA = [sb("SAf", [HALF, W2 + 1]), sb("SAb", [HALF, W2 + 1])]
        top, own = sb("top", [HALF, W2]), sb("own", [HALF, W2])
        AFTER = (slice(1, W2 + 1), slice(0, W2))
        BEFORE = (slice(0, W2), slice(1, W2 + 1))
        z_hi, z_lo = sb("z_hi", [HALF, 2, N], F32R), sb("z_lo", [HALF, 2, N], F32R)
        act, hid = sb("act", [128, 2, N]), sb("hid", [128, 1, N])
        hid_hi, hid_lo = sb("hid_hi", [128, 2, N], F32R), sb("hid_lo", [128, 2, N], F32R)
        gate_r = sb("gate_r", [TP, TILES, C])
        sc, sfc, tmp_e, sel_e, eqs = (sb(n, [TP, TILES, EXPERTS]) for n in ("sc", "sfc", "tmp_e", "sel_e", "eqs"))
        pa, pb2, pc, pd = (sb(n, [TP, TILES, EGROUPS]) for n in ("pa", "pb2", "pc", "pd"))
        cmp1, cmp2 = (sb(n, [TP, TILES, EGROUPS, EGROUPS]) for n in ("cmp1", "cmp2"))
        top8 = sb("top8", [TP, TILES, 8])
        cnt = sb("cnt", [TP, TILES])
        c48 = sb("c48", [TP, TILES, CROWS], F32R)
        cT = sb("cT", [CROWS, N], F32R)

        PF = pb("PF", [128, 2, 512])
        PG = pb("PG", [128, 2, 2, 512])
        PA = pb("PA", [128, 2, 512])

        raw_in = [sem(f"raw_in{i}") for i in range(RING)]
        hi_done, lo_done = sem("hi_done"), sem("lo_done")
        consts_in = sem("consts_in")
        consts_done = sem("consts_done")
        setup_v = sem("setup_v")
        pat_in = counted("pat_in", 16)
        pat_split = counted("pat_split", 2)
        pe_tok = counted("pe_tok", 1)
        tok_out = counted("tok_out", 2)
        split_ready = counted("split_ready", 3)
        pe_transposed = counted("pe_transposed", 9)
        act_stack = counted("act_stack", 9)
        pe_kvr = counted("pe_kvr", 3)
        act_kvr = counted("act_kvr", 3)
        exp_in = counted("exp_in", 5)
        exp_out = counted("exp_out", 7)
        z_ready = counted("z_ready", 1)
        pe_o = counted("pe_o", 1)
        o_used = counted("o_used", 1)
        pe_up = counted("pe_up", UPS)
        act_relu = counted("act_relu", UPS)
        hid_ready = counted("hid_ready", UPS + SCH + ECH)
        pe_down = counted("pe_down", UPS + SCH + ECH)
        pe_rf = counted("pe_rf", 1)
        act_rf = counted("act_rf", 1)
        kv_used = counted("kv_used", 1)
        pe_router = counted("pe_router", 1)
        act_sc = counted("act_sc", 1)
        logits_used = counted("logits_used", 1)
        sc_ready = counted("sc_ready", 1)
        c_ready = counted("c_ready", 1)
        pe_cT = counted("pe_cT", 1)
        act_cT = counted("act_cT", 1)
        pe_gu = counted("pe_gu", SCH + ECH)
        act_silu = counted("act_silu", SCH + ECH)
        gu_used = counted("gu_used", SCH + ECH)
        out_ready = counted("out_ready", 2)
        out_stored = counted("out_stored", 16 * TILES)
        dve = counted("dve", DVE_STEPS)
        block = ctx.enter_context(nc.Block())

        BANKS = ((0, 0, 2), (1, 2, 3))

        def rows(P, bank, a, b):
            return P[0:TP, bank, 0:(b - a) * C].rearrange("p (t c) -> p t c", c=C)

        def tile_out(P, t):
            return P[0:TP, t // 2, (t % 2) * C:(t % 2 + 1) * C]

        def halves(P):
            return P[0:HALF, :, 0:N]

        def two(x):
            return x[:, 0:W2].rearrange("p (h n) -> p h n", h=2)

        @block.sync
        def _(sp):
            def piece(n):
                name, prt, slots, cols, _ = PIECES[n]
                if n >= RING:
                    sp.wait_ge(lo_done, n - RING + 1)
                sp.dma_start(raw[n % RING][0:prt, 0:slots * cols],
                             A[f"w_{name}"]).then_inc(raw_in[n % RING], 16)

            piece(0)
            sp.dma_start(pat[:, :, :], A["patches"][0]).then_inc(pat_in, 16)
            for n in range(1, len(PIECES)):
                piece(n)
            def store(g):
                sp.wait_ge(out_ready, at(out_ready, g, 2))
                for t in range(TILES):
                    skip = TS[t - 1] + TP - TS[t] if t else 0
                    sp.dma_start(A["out"][bass.ds(g, 1), TS[t] + skip:TS[t] + TP, :].rearrange("a p c -> (a p) c"),
                                 h1[skip:TP, t, :]).then_inc(out_stored, 16)

            with sp.Fori(0, GROUPS - 1) as g:
                sp.wait_ge(pat_split, at(pat_split, g, 2))
                sp.dma_start(pat[:, :, :], A["patches"][bass.ds(g + 1, 1)].rearrange("a p k n -> (a p) k n")).then_inc(pat_in, 16)
                store(g)
            store(GROUPS - 1)
            sp.wait_ge(out_stored, at(out_stored, GROUPS, 0))

        @block.gpsimd
        def _(pool):
            def lo_part(n):
                name, prt, slots, cols, has_lo = PIECES[n]
                src = raw[n % RING][0:prt, 0:slots * cols].rearrange("p (s c) -> p s c", s=slots)
                pool.wait_ge(hi_done, n + 1)
                if n:
                    pool.wait_ge(lo_done, n)
                if name == "bd":
                    low = slice(2 * EXPERTS, CROWS)
                    nc.gpsimd.tensor_tensor(hi[name][low, :, :], src[low], hi[name][low, :, :].bitcast(F32),
                                            ALU.subtract).then_inc(lo_done, 1)
                    return
                if not has_lo:
                    nc.gpsimd.memset(nothing[:, n:n + 1], 0.0).then_inc(lo_done, 1)
                    return
                nc.gpsimd.tensor_tensor(lo[name][:, :, :], src, hi[name][:, 0:slots, :].bitcast(F32),
                                        ALU.subtract).then_inc(lo_done, 1)

            for n in range(len(PIECES)):
                lo_part(n)

        def act_group(actor, g):
            def stacks(first_n):
                for n in range(first_n, first_n + 3):
                    actor.wait_ge(pe_transposed, at(pe_transposed, g, n + 1))
                    nc.scalar.activation(stack[n // 3][:, n % 3, :], PF[:, n % 2, 0:N], ACT.Copy).then_inc(act_stack, 1)

            stacks(0)
            for n, (dst, f, s) in enumerate(((K, ACT.Copy, 1.0), (V, ACT.Copy, 1.0), (R, ACT.Exp, -1.0))):
                actor.wait_ge(pe_kvr, at(pe_kvr, g, n + 1))
                nc.scalar.activation(two(dst), halves(PF), f, scale=s).then_inc(act_kvr, 1)
            steps = [(E1[d][:, :], SB[d][:, AFTER[d]]) for d in range(2)]
            steps += [(M[d][:, BEFORE[d]],) for d in range(2)] + [(own[:, :],)]
            for n, arrays in enumerate(steps):
                actor.wait_ge(exp_in, at(exp_in, g, n + 1))
                for a in arrays:
                    nc.scalar.activation(a, a, ACT.Exp).then_inc(exp_out, 1)
            stacks(3)
            actor.wait_ge(pe_rf, at(pe_rf, g, 1))
            for bank, a, b in BANKS:
                last = nc.scalar.activation(gate_r[:, a:b, :], rows(PF, bank, a, b), ACT.Tanh, scale=0.5)
            last.then_inc(act_rf, 1)
            for m in range(UPS):
                actor.wait_ge(pe_up, at(pe_up, g, m + 1))
                if m >= 2:
                    actor.wait_ge(hid_ready, at(hid_ready, g, m - 1))
                nc.scalar.activation(act[:, m % 2, :], PG[:, m % 2, 0, 0:N], ACT.Relu).then_inc(act_relu, 1)
            stacks(6)
            actor.wait_ge(sc_ready, at(sc_ready, g, 1))
            nc.scalar.activation(sc[:, :, :], sc[:, :, :], ACT.Tanh, scale=0.5).then_inc(act_sc, 1)

            def silu(n):
                prt, bias = (INNER, sgb[:, n:n + 1]) if n < SCH else (128, egb[:, n - SCH:n - SCH + 1])
                actor.wait_ge(pe_gu, at(pe_gu, g, n + 1))
                if n >= 2:
                    actor.wait_ge(gu_used, at(gu_used, g, n - 1))
                nc.scalar.activation(act[0:prt, n % 2, :], PG[0:prt, n % 2, 0, 0:N], ACT.Silu,
                                     bias=bias).then_inc(act_silu, 1)

            for n in range(SCH):
                silu(n)
            actor.wait_ge(pe_cT, at(pe_cT, g, 1))
            nc.scalar.activation(cT[:, :], PF[0:CROWS, 1, 0:N], ACT.Copy).then_inc(act_cT, 1)
            for n in range(SCH, SCH + ECH):
                silu(n)

        @block.scalar
        def _(actor):
            loads = [(ident32[:, :], A["ident"])]
            for dst, src in ((ln1w, "ln1_w"), (ln1b, "ln1_b"), (ln2w, "ln2_w"), (ln2b, "ln2_b"), (sbd, "sbd")):
                loads.append((dst[:, :], A[src].broadcast_to([TP, C])))
            loads += [(rbias[:, :], A["router_b"].broadcast_to([TP, EXPERTS])),
                      (cbias[:, :], A["corr_bias"].broadcast_to([TP, EXPERTS])),
                      (before[:, :, :].rearrange("p i j -> p (i j)"), A["before"].broadcast_to([TP, EGROUPS * EGROUPS])),
                      (decay[:, :], A["decay"]), (first[:, :], A["first"]),
                      (egb[:, :], A["egb"]), (eub[:, :], A["eub"]), (sgb[:, :], A["sgb"]), (sub_[:, :], A["sub"])]
            assert len(loads) == N_CONST_LOADS
            for dst, src in loads:
                actor.dma_start(dst, src).then_inc(consts_in, 16)
            actor.wait_ge(consts_done, 1)
            for b in range(IMGS):
                for t in range(TILES):
                    if 0 <= b * T - TS[t] < TP:
                        actor.dma_start(cls_rows[b * T - TS[t]:b * T - TS[t] + 1, t, :], A["cls"]).then_inc(consts_in, 16)

            def hi_part(n):
                name, prt, slots, cols, _ = PIECES[n]
                actor.wait_ge(raw_in[n % RING], 16 * (n // RING + 1))
                nc.scalar.activation(hi[name][:, :, :], raw[n % RING][0:prt, 0:slots * cols].rearrange("p (s c) -> p s c", s=slots),
                                     ACT.Copy).then_inc(hi_done, 1)

            for n in range(len(PIECES)):
                hi_part(n)
            with actor.Fori(0, GROUPS) as g:
                act_group(actor, g)

        def dve_group(v, g):
            V_ = nc.vector
            count, spares = [0], [0]

            def step(ins):
                count[0] += 1
                ins.then_inc(dve, 1)

            def settle():
                v.wait_ge(dve, at(dve, g, count[0]))

            def do(ins):
                step(ins)
                settle()

            def settle_apart():
                settle()
                V_.memset(spare_v[:, spares[0]:spares[0] + 1], 0.0)
                spares[0] += 1

            def rsqrt(cols):
                a, r, y = var[:, 0:cols, :], rstd[:, 0:cols, :], ny[:, 0:cols, :]
                s = seed[:, 0:cols, :]
                do(V_.tensor_scalar(s, a.bitcast(I32), 1, None, ALU.logical_shift_right))
                do(V_.tensor_scalar(r.bitcast(I32), s, -1.0, RSQRT_SEED, ALU.mult, ALU.add))
                for _ in range(4):
                    do(V_.tensor_tensor(y, r, r, ALU.mult))
                    do(V_.scalar_tensor_tensor(y, y, -0.5, a, ALU.mult, ALU.mult))
                    do(V_.scalar_tensor_tensor(r, y, 1.5, r, ALU.add, ALU.mult))

            def moments(x):
                for t in range(TILES):
                    step(V_.bn_stats(stats[:, t, :], x[:, t, :]))
                settle_apart()
                for t in range(TILES):
                    step(V_.bn_aggr(mv[:, t, :], stats[:, t, :]))
                settle()

            def normalise(dst, x):
                for t in range(TILES):
                    step(V_.tensor_scalar(dst[:, t, :], x[:, t, :], mv[:, t, 0:1], rstd[:, 0, t:t + 1],
                                             ALU.subtract, ALU.mult))
                settle()

            def affine(w, b):
                do(V_.tensor_tensor(norm[:, :, :], norm[:, :, :], w[:, None, :].broadcast_to([TP, TILES, C]), ALU.mult))
                do(V_.tensor_tensor(norm[:, :, :], norm[:, :, :], b[:, None, :].broadcast_to([TP, TILES, C]), ALU.add))

            def split_rows(x, n):
                if n:
                    v.wait_ge(pe_transposed, at(pe_transposed, g, 3 * n))
                do(V_.tensor_copy(split[:, :, 0:C], x[:, :, :]))
                step(V_.tensor_tensor(split[:, :, C:256], x[:, :, 128:C], split[:, :, 128:C].bitcast(F32), ALU.subtract))
                V_.tensor_tensor(split[:, :, 256:384], x[:, :, 0:128], split[:, :, 0:128].bitcast(F32),
                                 ALU.subtract).then_inc(split_ready, 1)
                settle()

            v.wait_ge(pat_in, at(pat_in, g, 16))
            V_.tensor_copy(pat_hi[:, :, :], pat[:, :, :]).then_inc(pat_split, 1)
            v.wait_ge(pat_split, at(pat_split, g, 1))
            V_.tensor_tensor(pat_lo[:, :, :], pat[:, :, :], pat_hi[:, :, :].bitcast(F32), ALU.subtract).then_inc(pat_split, 1)
            v.wait_ge(pe_tok, at(pe_tok, g, 1))
            for bank, a, b in BANKS:
                V_.tensor_tensor(h0[:, a:b, :], rows(PF, bank, a, b), cls_rows[:, a:b, :], ALU.add).then_inc(tok_out, 1)
            v.wait_ge(tok_out, at(tok_out, g, 2))
            moments(h0)
            vv = mv[:, :, 1]
            do(V_.tensor_scalar(var[:, 0, :], vv, EPS, None, ALU.add))
            do(V_.reciprocal(var[:, 1, :], var[:, 0, :]))
            do(V_.tensor_tensor(var[:, 1, :], var[:, 1, :], vv, ALU.mult))
            do(V_.tensor_scalar(var[:, 1, :], var[:, 1, :], EPS, None, ALU.add))
            rsqrt(2)
            normalise(x0, h0)
            for t in range(TILES):
                step(V_.tensor_scalar(norm[:, t, :], x0[:, t, :], rstd[:, 1, t:t + 1], None, ALU.mult))
            settle()
            affine(ln1w, ln1b)
            split_rows(norm, 0)

            v.wait_ge(act_kvr, at(act_kvr, g, 1))
            def run(x, d):
                return x if d == 0 else x[:, ::-1]

            for d, dec in enumerate((dec_f, dec_b)):
                do(V_.tensor_tensor_scan(run(M[d][:, AFTER[d]], d), run(dec[:, :], d), run(K[:, :], d), 0.0, ALU.add, ALU.max))
            for d in range(2):
                old, new = M[d][:, BEFORE[d]], M[d][:, AFTER[d]]
                for h in range(2):
                    s = slice(h * N, (h + 1) * N)
                    step(V_.scalar_tensor_tensor(E1[d][:, s], old[:, s], decay[:, h:h + 1], new[:, s], ALU.add, ALU.subtract))
                do(V_.tensor_tensor(SB[d][:, AFTER[d]], K[:, :], new, ALU.subtract))
                start = 0 if d == 0 else T - 1
                do(V_.memset(old[:, start::T], NEG))
                V_.memset(E1[d][:, start::T], NEG).then_inc(exp_in, 1)
            mf, mb = M[0][:, BEFORE[0]], M[1][:, BEFORE[1]]
            do(V_.tensor_tensor(top[:, :], mf, mb, ALU.max))
            for h in range(2):
                s = slice(h * N, (h + 1) * N)
                step(V_.scalar_tensor_tensor(top[:, s], K[:, s], first[:, h:h + 1], top[:, s], ALU.add, ALU.max))
            settle()
            V_.tensor_tensor(mf, mf, top[:, :], ALU.subtract).then_inc(exp_in, 1)
            V_.tensor_tensor(mb, mb, top[:, :], ALU.subtract).then_inc(exp_in, 1)
            do(V_.scalar_tensor_tensor(own[:, 0:N], K[:, 0:N], first[:, 0:1], top[:, 0:N], ALU.add, ALU.subtract))
            V_.scalar_tensor_tensor(own[:, N:W2], K[:, N:W2], first[:, 1:2], top[:, N:W2], ALU.add, ALU.subtract).then_inc(exp_in, 1)
            v.wait_ge(act_kvr, at(act_kvr, g, 2))
            for d in range(2):
                v.wait_ge(exp_out, at(exp_out, g, 2 * d + 2))
                a, b = SA[d][:, AFTER[d]], SB[d][:, AFTER[d]]
                do(V_.tensor_tensor(a, b, V[:, :], ALU.mult))
                step(V_.tensor_tensor_scan(run(a, d), run(E1[d][:, :], d), run(a, d), 0.0, ALU.mult, ALU.add))
                do(V_.tensor_tensor_scan(run(b, d), run(E1[d][:, :], d), run(b, d), 0.0, ALU.mult, ALU.add))
            for d in range(2):
                v.wait_ge(exp_out, at(exp_out, g, 5 + d))
                for x in (SA[d], SB[d]):
                    step(V_.tensor_tensor(x[:, BEFORE[d]], x[:, BEFORE[d]], M[d][:, BEFORE[d]], ALU.mult))
            v.wait_ge(exp_out, at(exp_out, g, 7))
            do(V_.tensor_tensor(V[:, :], V[:, :], own[:, :], ALU.mult))
            step(V_.tensor_tensor(top[:, :], SA[0][:, BEFORE[0]], SA[1][:, BEFORE[1]], ALU.add))
            do(V_.tensor_tensor(K[:, :], SB[0][:, BEFORE[0]], SB[1][:, BEFORE[1]], ALU.add))
            step(V_.tensor_tensor(top[:, :], top[:, :], V[:, :], ALU.add))
            do(V_.tensor_tensor(K[:, :], K[:, :], own[:, :], ALU.add))
            v.wait_ge(act_kvr, at(act_kvr, g, 3))
            do(V_.scalar_tensor_tensor(K[:, :], R[:, :], 1.0, K[:, :], ALU.add, ALU.mult))
            do(V_.reciprocal(K[:, :], K[:, :]))
            do(V_.tensor_tensor(K[:, :], K[:, :], top[:, :], ALU.mult))
            do(V_.tensor_copy(z_hi[:, :, :], two(K)))
            V_.tensor_tensor(z_lo[:, :, :], two(K), z_hi[:, :, :].bitcast(F32), ALU.subtract).then_inc(z_ready, 1)

            v.wait_ge(pe_o, at(pe_o, g, 1))
            for bank, a, b in BANKS:
                step(V_.tensor_tensor(x0[:, a:b, :], x0[:, a:b, :], rows(PF, bank, a, b), ALU.add))
            settle()
            moments(x0)
            do(V_.tensor_scalar(var[:, 0, :], vv, EPS, None, ALU.add))
            rsqrt(1)
            normalise(norm, x0)
            affine(ln2w, ln2b)
            split_rows(norm, 1)

            def split_hidden(prt, i):
                do(V_.tensor_copy(hid_hi[0:prt, i, :], hid[0:prt, 0, :]))
                V_.tensor_tensor(hid_lo[0:prt, i, :], hid[0:prt, 0, :], hid_hi[0:prt, i, :].bitcast(F32),
                                 ALU.subtract).then_inc(hid_ready, 1)

            for m in range(UPS):
                v.wait_ge(act_relu, at(act_relu, g, m + 1))
                if m:
                    v.wait_ge(hid_ready, at(hid_ready, g, m))
                do(V_.tensor_tensor(hid[:, 0, :], act[:, m % 2, :], act[:, m % 2, :], ALU.mult))
                if m >= 2:
                    v.wait_ge(pe_down, at(pe_down, g, m - 1))
                split_hidden(128, m % 2)
            v.wait_ge(act_rf, at(act_rf, g, 1))
            v.wait_ge(pe_down, at(pe_down, g, UPS))
            for bank, a, b in BANKS:
                step(V_.scalar_tensor_tensor(gate_r[:, a:b, :], gate_r[:, a:b, :], 1.0, rows(PA, bank, a, b), ALU.add, ALU.mult))
            settle()
            do(V_.scalar_tensor_tensor(x0[:, :, :], gate_r[:, :, :], 0.5, x0[:, :, :], ALU.mult, ALU.add))
            V_.tensor_tensor(h1[:, :, :], h0[:, :, :], x0[:, :, :], ALU.add).then_inc(kv_used, 1)
            v.wait_ge(kv_used, at(kv_used, g, 1))

            moments(h1)
            do(V_.tensor_scalar(var[:, 0, :], vv, EPS, None, ALU.add))
            rsqrt(1)
            normalise(norm, h1)
            split_rows(norm, 2)
            do(V_.tensor_tensor(h1[:, :, :], h1[:, :, :], sbd[:, None, :].broadcast_to([TP, TILES, C]), ALU.add))
            v.wait_ge(pe_router, at(pe_router, g, 1))
            E3 = [TP, TILES, EXPERTS]
            V_.tensor_tensor(sc[:, :, :], PF[0:TP, 0, 0:TILES * EXPERTS].rearrange("p (t e) -> p t e", e=EXPERTS),
                             rbias[:, None, :].broadcast_to(E3), ALU.add).then_inc(sc_ready, 1)
            v.wait_ge(act_sc, at(act_sc, g, 1))
            do(V_.tensor_scalar(sc[:, :, :], sc[:, :, :], 1.0, 0.5, ALU.add, ALU.mult))
            do(V_.tensor_tensor(sfc[:, :, :], sc[:, :, :], cbias[:, None, :].broadcast_to(E3), ALU.add))
            quad = sfc[:, :, :].rearrange("p t (g e) -> p t g e", e=EPG)
            q = [quad[:, :, :, i] for i in range(EPG)]
            P_, S_ = tmp_e[:, :, 0:EGROUPS], tmp_e[:, :, EGROUPS:2 * EGROUPS]
            step(V_.tensor_tensor(pa[:, :, :], q[0], q[1], ALU.max))
            step(V_.tensor_tensor(pb2[:, :, :], q[0], q[1], ALU.min))
            step(V_.tensor_tensor(pc[:, :, :], q[2], q[3], ALU.max))
            step(V_.tensor_tensor(pd[:, :, :], q[2], q[3], ALU.min))
            settle()
            step(V_.tensor_tensor(P_, pa[:, :, :], pc[:, :, :], ALU.max))
            step(V_.tensor_tensor(S_, pa[:, :, :], pc[:, :, :], ALU.min))
            do(V_.tensor_tensor(pb2[:, :, :], pb2[:, :, :], pd[:, :, :], ALU.max))
            do(V_.tensor_tensor(S_, S_, pb2[:, :, :], ALU.max))
            do(V_.tensor_tensor(pa[:, :, :], P_, S_, ALU.add))
            G4 = [TP, TILES, EGROUPS, EGROUPS]
            other, mine = pa[:, :, None, :].broadcast_to(G4), pa[:, :, :, None].broadcast_to(G4)
            step(V_.tensor_tensor(cmp1[:, :, :, :], other, mine, ALU.is_gt))
            do(V_.tensor_tensor(cmp2[:, :, :, :], other, mine, ALU.is_equal))
            do(V_.tensor_tensor(cmp2[:, :, :, :], cmp2[:, :, :, :], before[:, None, :, :].broadcast_to(G4), ALU.mult))
            do(V_.tensor_tensor(cmp1[:, :, :, :], cmp1[:, :, :, :], cmp2[:, :, :, :], ALU.add))
            do(V_.tensor_reduce(pa[:, :, :], cmp1[:, :, :, :], AXX, ALU.add))
            do(V_.tensor_scalar(pa[:, :, :], pa[:, :, :], float(TOPG), None, ALU.is_lt))
            step(V_.tensor_tensor(quad, quad, pa[:, :, :, None].broadcast_to([TP, TILES, EGROUPS, EPG]), ALU.mult))
            settle_apart()
            for t in range(TILES):
                step(V_.max(top8[:, t, :], sfc[:, t, :]))
            settle()
            fourth = top8[:, :, TOPK - 1:TOPK].broadcast_to(E3)
            step(V_.tensor_tensor(sel_e[:, :, :], sfc[:, :, :], fourth, ALU.is_gt))
            do(V_.tensor_tensor(eqs[:, :, :], sfc[:, :, :], fourth, ALU.is_equal))
            do(V_.tensor_reduce(cnt[:, :], sel_e[:, :, :], AXX, ALU.add))
            for t in range(TILES):
                step(V_.tensor_tensor_scan(tmp_e[:, t, :], ones_e[:, :], eqs[:, t, :], cnt[:, t:t + 1], ALU.mult, ALU.add))
            settle()
            do(V_.scalar_tensor_tensor(tmp_e[:, :, :], tmp_e[:, :, :], float(TOPK), eqs[:, :, :], ALU.is_le, ALU.mult))
            do(V_.tensor_tensor(sel_e[:, :, :], sel_e[:, :, :], tmp_e[:, :, :], ALU.add))
            do(V_.tensor_tensor(sc[:, :, :], sc[:, :, :], sel_e[:, :, :], ALU.mult))
            do(V_.tensor_reduce(cnt[:, :], sc[:, :, :], AXX, ALU.add))
            do(V_.tensor_scalar(cnt[:, :], cnt[:, :], 1e-20, None, ALU.add))
            do(V_.reciprocal(cnt[:, :], cnt[:, :]))
            do(V_.scalar_tensor_tensor(sc[:, :, :], sc[:, :, :], SCALE, cnt[:, :, None].broadcast_to(E3), ALU.mult, ALU.mult))
            step(V_.tensor_copy(c48[:, :, 0:EXPERTS], sc[:, :, :]))
            do(V_.tensor_copy(c48[:, :, 2 * EXPERTS:3 * EXPERTS], sc[:, :, :]))
            V_.tensor_tensor(c48[:, :, EXPERTS:2 * EXPERTS], sc[:, :, :], c48[:, :, 0:EXPERTS].bitcast(F32),
                             ALU.subtract).then_inc(c_ready, 1)

            for n in range(SCH + ECH):
                i, prt = n % 2, INNER if n < SCH else 128
                v.wait_ge(act_silu, at(act_silu, g, n + 1))
                if n < SCH:
                    bias = sub_[:, n:n + 1]
                else:
                    bias = eub[:, n - SCH:n - SCH + 1]
                    do(V_.tensor_tensor(act[:, i, :].rearrange("p (h n) -> p h n", h=2),
                                           act[:, i, :].rearrange("p (h n) -> p h n", h=2),
                                           PG[:, i, :, N:N + N // 2], ALU.mult))
                v.wait_ge(hid_ready, at(hid_ready, g, UPS + n))
                V_.scalar_tensor_tensor(hid[0:prt, 0, :], PG[0:prt, i, 1, 0:N], bias, act[0:prt, i, :],
                                        ALU.add, ALU.mult).then_inc(gu_used, 1)
                v.wait_ge(gu_used, at(gu_used, g, n + 1))
                if n >= 2:
                    v.wait_ge(pe_down, at(pe_down, g, UPS + n - 1))
                split_hidden(prt, i)
            v.wait_ge(pe_down, at(pe_down, g, UPS + SCH + ECH))
            for bank, a, b in BANKS:
                V_.tensor_tensor(h1[:, a:b, :], h1[:, a:b, :], rows(PA, bank, a, b), ALU.add).then_inc(out_ready, 1)
            v.wait_ge(out_stored, at(out_stored, g, 16 * TILES))
            assert count[0] == per_group[dve], count

        @block.vector
        def _(v):
            count = [0]

            def setup(ins):
                count[0] += 1
                ins.then_inc(setup_v, 1)

            nc.vector.memset(cls_rows[:, :, :], 0.0).then_inc(consts_done, 1)
            for d in range(2):
                edge = 0 if d == 0 else W2
                for a in (M[d], SA[d], SB[d]):
                    setup(nc.vector.memset(a[:, edge:edge + 1], 0.0))
            setup(nc.vector.memset(own[:, :], 0.0))
            setup(nc.vector.memset(ones_e[:, :], 1.0))
            v.wait_ge(consts_in, 16 * (N_CONST_LOADS + N_CLS))
            setup(nc.vector.tensor_copy(ident[:, :], ident32[:, :]))
            setup(nc.vector.tensor_scalar(decay[:, :], decay[:, :], 1.0 / T, None, ALU.mult))
            setup(nc.vector.tensor_scalar(first[:, :], first[:, :], 1.0 / T, None, ALU.mult))
            v.wait_ge(setup_v, count[0])
            for a in (dec_f, dec_b):
                for h in range(2):
                    setup(nc.vector.tensor_scalar(a[:, h * N:(h + 1) * N], own[:, 0:N], decay[:, h:h + 1], None, ALU.add))
            v.wait_ge(setup_v, count[0])
            setup(nc.vector.memset(dec_f[:, 0:W2:T], NEG))
            nc.vector.memset(dec_b[:, T - 1:W2:T], NEG).then_inc(consts_done, 1)
            v.wait_ge(setup_v, count[0])
            v.wait_ge(consts_done, 2)
            with v.Fori(0, GROUPS) as g:
                dve_group(v, g)

        def pe_group(pe, g):
            mm = nc.tensor.matmul

            def need(name):
                pe.wait_ge(lo_done, PIECE_AT[name] + 1)

            def transposes(n):
                pe.wait_ge(split_ready, at(split_ready, g, n + 1))
                for p in range(3):
                    k = 3 * n + p
                    if p == 2:
                        pe.wait_ge(act_stack, at(act_stack, g, k - 1))
                    for t in range(TILES):
                        last = nc.tensor.transpose(PF[:, k % 2, TS[t]:TS[t] + TP].bitcast(F32R),
                                                   split[:, t, p * 128:(p + 1) * 128], ident[0:TP, 0:TP])
                    last.then_inc(pe_transposed, 1)

            def from_stack(out, n, name, cols):
                w_hi, w_lo = hi[name], lo[name]
                for p, slot in enumerate((0, 1, 0)):
                    mm(out, w_hi[:, slot, cols], stack[n][:, p, :], start=(p == 0), stop=False)
                for p in range(2):
                    last = mm(out, w_lo[:, p, cols], stack[n][:, p, :], start=False, stop=(p == 1))
                return last

            def rows_from_stack(P, n, name, cols, place):
                w_hi, w_lo = hi[name], lo[name]
                for t in range(TILES):
                    out = place(P, t)
                    for p, slot in enumerate((0, 1, 0)):
                        mm(out, stack[n][:, p, TS[t]:TS[t] + TP], w_hi[:, slot, cols],
                           start=(p == 0 and opens(place, t)), stop=False, skip_group_check=True)
                    for p in range(2):
                        last = mm(out, stack[n][:, p, TS[t]:TS[t] + TP], w_lo[:, p, cols],
                                  start=False, stop=(p == 1), skip_group_check=True)
                return last

            def opens(place, t):
                return t == 0 if place is router_out else t != 1

            def router_out(P, t):
                return P[0:TP, 0, t * EXPERTS:(t + 1) * EXPERTS]

            def down(P, src_hi, src_lo, w_hi, w_lo, start, stop):
                for t in range(TILES):
                    s = slice(TS[t], TS[t] + TP)
                    mm(tile_out(P, t), src_hi[:, s], w_hi, start=start and t != 1, stop=False, skip_group_check=True)
                    mm(tile_out(P, t), src_hi[:, s], w_lo, start=False, stop=False, skip_group_check=True)
                    last = mm(tile_out(P, t), src_lo[:, s], w_hi, start=False, stop=stop, skip_group_check=True)
                return last

            need("tok")
            pe.wait_ge(pat_split, at(pat_split, g, 2))
            for k in range(2):
                last = down(PF, pat_hi[:, k, :], pat_lo[:, k, :], hi["tok"][:, k, :], lo["tok"][:, k, :], k == 0, k == 1)
            last.then_inc(pe_tok, 1)
            pe.wait_ge(tok_out, at(tok_out, g, 2))
            transposes(0)
            for n, name in enumerate(("k", "v", "r")):
                need(name)
                if n == 0:
                    pe.wait_ge(act_stack, at(act_stack, g, 3))
                else:
                    pe.wait_ge(act_kvr, at(act_kvr, g, n))
                for h in range(2):
                    last = from_stack(PF[0:HALF, h, 0:N], 0, name, slice(h * HALF, (h + 1) * HALF))
                last.then_inc(pe_kvr, 1)
            need("o")
            pe.wait_ge(z_ready, at(z_ready, g, 1))
            for h in range(2):
                last = down(PF, z_hi[:, h, :], z_lo[:, h, :], hi["o"][:, h, :], lo["o"][:, h, :], h == 0, h == 1)
            last.then_inc(pe_o, 1)
            transposes(1)
            pe.wait_ge(act_stack, at(act_stack, g, 6))
            need("rf")
            rows_from_stack(PF, 1, "rf", slice(0, C), tile_out).then_inc(pe_rf, 1)

            def up(m):
                need(f"up{m // 3}")
                if m >= 2:
                    pe.wait_ge(act_relu, at(act_relu, g, m - 1))
                from_stack(PG[:, m % 2, 0, 0:N], 1, f"up{m // 3}", slice(m % 3 * 128, (m % 3 + 1) * 128)).then_inc(pe_up, 1)

            def mix(m):
                w, j = f"down{m // 3}", m % 3
                need(w)
                pe.wait_ge(hid_ready, at(hid_ready, g, m + 1))
                down(PA, hid_hi[:, m % 2, :], hid_lo[:, m % 2, :], hi[w][:, j, :], lo[w][:, j, :],
                     m == 0, m == UPS - 1).then_inc(pe_down, 1)

            up(0)
            for m in range(UPS):
                if m + 1 < UPS:
                    up(m + 1)
                mix(m)
            transposes(2)
            pe.wait_ge(act_stack, at(act_stack, g, 9))
            need("router")
            rows_from_stack(PF, 2, "router", slice(0, EXPERTS), router_out).then_inc(pe_router, 1)

            def gate_up(n):
                i = n % 2
                if n >= 2:
                    pe.wait_ge(gu_used, at(gu_used, g, n - 1))
                if n < SCH:
                    name, base, width = "sgu", n * 2 * INNER, INNER
                    need(name)
                else:
                    j = n - SCH
                    name, base, width = f"egu{j // 2}", (j % 2) * 256, 128
                    need(name)
                    for u in range(2):
                        mm(PG[:, i, u, N:N + N // 2], hi[f"sel{j // 6}"][:, j % 6, :],
                           cT[:, u * (N // 2):(u + 1) * (N // 2)], start=True, stop=True)
                for u in range(2):
                    last = from_stack(PG[0:width, i, u, 0:N], 2, name, slice(base + u * width, base + (u + 1) * width))
                last.then_inc(pe_gu, 1)

            def expert_down(n):
                i = n % 2
                pe.wait_ge(hid_ready, at(hid_ready, g, UPS + n + 1))
                if n < SCH:
                    need("sd")
                    s = slice(0, INNER)
                    w_hi, w_lo = hi["sd"][:, n, :], lo["sd"][:, n, :]
                else:
                    j = n - SCH
                    name = f"ed{j // 4}"
                    need(name)
                    s = slice(0, 128)
                    w_hi, w_lo = hi[name][:, j % 4, :], lo[name][:, j % 4, :]
                down(PA, hid_hi[s, i, :], hid_lo[s, i, :], w_hi, w_lo, n == 0, n == SCH + ECH - 1).then_inc(pe_down, 1)

            pe.wait_ge(kv_used, at(kv_used, g, 1))
            gate_up(0)
            gate_up(1)
            expert_down(0)
            pe.wait_ge(c_ready, 1)
            pe.wait_ge(c_ready, at(c_ready, g, 1))
            for t in range(TILES):
                last = nc.tensor.transpose(PF[0:CROWS, 1, TS[t]:TS[t] + TP].bitcast(F32R), c48[:, t, :], ident[0:TP, 0:TP])
            last.then_inc(pe_cT, 1)
            pe.wait_ge(act_cT, at(act_cT, g, 1))
            need("bd")
            need("sel1")
            for n in range(2, SCH + ECH):
                gate_up(n)
                if n == 2:
                    for t in range(TILES):
                        mm(tile_out(PA, t), cT[:, TS[t]:TS[t] + TP], hi["bd"][:, 0, :],
                           start=False, stop=False, skip_group_check=True)
                expert_down(n - 1)
            expert_down(SCH + ECH - 1)

        @block.tensor
        def _(pe):
            pe.wait_ge(consts_done, 2)
            with pe.Fori(0, GROUPS) as g:
                pe_group(pe, g)


N_CONST_LOADS = 15
N_CLS = sum(0 <= b * T - t < TP for b in range(IMGS) for t in TS)
DVE_STEPS = 201


def _stack(w):
    import numpy as np
    wt = w.T
    return np.stack([wt[0:128], np.concatenate([wt[128:192]] * 2)], axis=1)


def kernel(**inputs):
    import numpy as np
    import concourse.bacc as bacc
    from concourse.bass_utils import run_bass_kernel_spmd

    I = {k: np.asarray(v) for k, v in inputs.items()}
    a = {}
    x = I["x"].reshape(GROUPS, IMGS, SIDE, PATCH, SIDE, PATCH).transpose(0, 3, 5, 1, 2, 4)
    pat = np.zeros((GROUPS, PIX, IMGS, T), np.float32)
    pat[..., 1:] = x.reshape(GROUPS, PIX, IMGS, SIDE * SIDE)
    a["patches"] = pat.reshape(GROUPS, 2, 128, N).transpose(0, 2, 1, 3)
    a["cls"] = I["cls_tok"].reshape(1, C)
    a["ident"] = np.eye(128, dtype=np.float32)
    p = np.arange(ECH * 128) // INNER
    sel = np.concatenate([(p == np.arange(EXPERTS)[:, None])] * 2 + [np.zeros((EXPERTS, ECH * 128), bool)]).astype(np.float32)
    a["w_sel0"], a["w_sel1"] = sel[:, :ECH * 64], sel[:, ECH * 64:]
    a["before"] = (np.arange(EGROUPS)[None, :] < np.arange(EGROUPS)[:, None]).astype(np.float32).reshape(1, -1)
    for n in ("ln1_w", "ln1_b", "ln2_w", "ln2_b"):
        a[n] = I["L0_attn_" + n].reshape(1, C)
    for n in ("router_b", "corr_bias", "sbd"):
        a[n] = I["L0_ffn_" + n].reshape(1, -1)
    for n in ("decay", "first"):
        a[n] = I["L0_attn_" + n].reshape(2, HALF).T
    a["egb"], a["eub"] = (I["L0_ffn_" + n].reshape(ECH, 128).T for n in ("gbg", "gbu"))
    a["sgb"], a["sub"] = (I["L0_ffn_" + n].reshape(SCH, INNER).T for n in ("sbg", "sbu"))
    a["w_tok"] = I["L0_tok_W"].T.reshape(2, 128, C).transpose(1, 0, 2)
    for n in ("k", "v", "r"):
        a[f"w_{n}"] = _stack(I[f"L0_attn_W{n}_a"])
    a["w_o"] = I["L0_attn_Wo_a"].T.reshape(2, HALF, C).transpose(1, 0, 2)
    up = _stack(I["L0_attn_Wk_f"])
    a["w_up0"], a["w_up1"] = up[:, :, :HID // 2], up[:, :, HID // 2:]
    a["w_rf"] = _stack(I["L0_attn_Wr_f"])
    down = I["L0_attn_Wv_f"].T.reshape(UPS, 128, C).transpose(1, 0, 2)
    a["w_down0"], a["w_down1"] = down[:, :UPS // 2], down[:, UPS // 2:]
    a["w_router"] = _stack(I["L0_ffn_router_w"])
    sg, su = _stack(I["L0_ffn_sWg"].T), _stack(I["L0_ffn_sWu"].T)
    a["w_sgu"] = np.stack([sg.reshape(128, 2, SCH, INNER), su.reshape(128, 2, SCH, INNER)], axis=3)
    a["w_sd"] = I["L0_ffn_sWd"].reshape(SCH, INNER, C).transpose(1, 0, 2)
    a["w_bd"] = np.concatenate([I["L0_ffn_gbd"]] * 3)
    eg, eu = (_stack(I["L0_ffn_" + n].transpose(0, 2, 1).reshape(EXPERTS * INNER, C)) for n in ("gWg", "gWu"))
    egu = np.stack([eg.reshape(128, 2, ECH // 2, 2, 128), eu.reshape(128, 2, ECH // 2, 2, 128)], axis=4)
    ed = I["L0_ffn_gWd"].reshape(3, 4, 128, C).transpose(0, 2, 1, 3)
    for i in range(ECH // 2):
        a[f"w_egu{i}"] = egu[:, :, i]
    for i in range(3):
        a[f"w_ed{i}"] = ed[i]
    for name, prt, slots, cols, _ in PIECES:
        a[f"w_{name}"] = a[f"w_{name}"].reshape(prt, slots * cols)

    nc = bacc.Bacc("TRN2", target_bir_lowering=False, num_devices=1, dynamic_dma_scratch_size=1024)
    arrays = {f"in_{k}": np.ascontiguousarray(x) for k, x in a.items()}
    A = {k: nc.dram_tensor(f"in_{k}", arrays[f"in_{k}"].shape, F32, kind="ExternalInput").ap() for k in a}
    A["out"] = nc.dram_tensor("out", (GROUPS, N, C), F32, kind="ExternalOutput").ap()
    build(nc, A)
    r = run_bass_kernel_spmd(nc, [arrays], core_ids=[0])
    return r.results[0]["out"].reshape(BATCH, T, C)
```

```python
from contextlib import ExitStack

import concourse.bass as bass
from concourse import mybir

F32, F32R, I32 = mybir.dt.float32, mybir.dt.float32r, mybir.dt.int32
ALU, ACT = mybir.AluOpType, mybir.ActivationFunctionType
AXX = mybir.AxisListType.X

BATCH, SIDE, PATCH, C = 32, 6, 16, 192
T = SIDE * SIDE + 1
PIX = PATCH * PATCH
GROUPS = 4
IMGS = BATCH // GROUPS
N = IMGS * T
TILES = 3
TP = -(-N // TILES // 2) * 2
TS = [0, (N - TP) // 4 * 2, N - TP]
HALF = C // 2
HID = 4 * C
UPS = HID // 128
EXPERTS, INNER, EGROUPS, TOPG, TOPK = 16, 96, 4, 2, 4
EPG = EXPERTS // EGROUPS
ECH = EXPERTS * INNER // 128
SCH = 2
SCALE = 2.5
EPS = 1e-5
NEG = -1e38
CROWS = 3 * EXPERTS
RSQRT_SEED = float(0x5F3759DF)
W2 = 2 * N
SEQS = 2 * IMGS

def _pieces():
    yield from ((m, 128, 2, C, True) for m in ("k", "v", "r", "rf"))
    yield from ((f"up{i}", 128, 2, HID // 2, True) for i in range(2))
    yield ("router", 128, 2, EXPERTS, True)
    yield ("sgu", 128, 2, 2 * C, True)
    yield ("bd", CROWS, 1, C, False)
    yield from ((f"sel{i}", CROWS, ECH // 2, 128, False) for i in range(2))
    yield from ((f"egu{i}", 128, 2, 512, True) for i in range(ECH // 2))


WHOLE = [("tok", 128, 2), ("o", HALF, 2), ("down", 128, UPS), ("sd", INNER, SCH), ("ed", 128, ECH)]
PIECES = list(_pieces())
PIECE_AT = {p[0]: n for n, p in enumerate(PIECES)}
RING, RING_COLS = 4, 2 * 512


def build(nc, A):
    ctx = ExitStack()
    with ctx:
        def sb(name, shape, dt=F32):
            return ctx.enter_context(nc.sbuf_tensor(name, shape, dt))

        def pb(name, shape):
            return ctx.enter_context(nc.psum_tensor(name, shape, F32))

        def sem(name):
            return ctx.enter_context(nc.semaphore(name))

        per_group, raised_before = {}, {}

        def counted(name, n, before_first=0):
            s = sem(name)
            per_group[s] = n
            raised_before[s] = before_first
            return s

        def at(s, g, n):
            return g * per_group[s] + (raised_before[s] + n)

        hi = {p[0]: sb(f"hi_{p[0]}", [p[1], p[2], p[3]], F32R) for p in PIECES}
        lo = {p[0]: sb(f"lo_{p[0]}", [p[1], p[2], p[3]], F32R) for p in PIECES if p[4]}
        whole = {name: sb(f"w_{name}", [p, n, C]) for name, p, n in WHOLE}
        raw = [sb(f"raw{i}", [128, RING_COLS]) for i in range(RING)]
        ident32, ident = sb("ident32", [128, 128]), sb("ident", [128, 128], F32R)
        ones_e = sb("ones_e", [TP, EXPERTS])
        cls_rows = sb("cls_rows", [TP, TILES, C])
        ln1w, ln1b = sb("ln1w", [TP, C]), sb("ln1b", [TP, C])
        ln2w, ln2b = sb("ln2w", [TP, C]), sb("ln2b", [TP, C])
        sbd = sb("sbd", [TP, C])
        rbias, cbias = sb("rbias", [TP, EXPERTS]), sb("cbias", [TP, EXPERTS])
        before = sb("before", [TP, EGROUPS, EGROUPS])
        decay, first = sb("decay", [HALF, 2]), sb("first", [HALF, 2])
        dec_f, dec_b = sb("dec_f", [HALF, W2]), sb("dec_b", [HALF, W2])
        egb, eub = sb("egb", [128, ECH]), sb("eub", [128, ECH])
        sgb, sub_ = sb("sgb", [INNER, SCH]), sb("sub_", [INNER, SCH])
        nothing, spare_v = sb("nothing", [128, len(PIECES)]), sb("spare_v", [128, 8])
        pat = sb("pat", [128, 2, N])
        h0, x0, norm = (sb(n, [TP, TILES, C]) for n in ("h0", "x0", "norm"))
        base, h1, gate_r, norm3 = (sb(n, [TP, TILES, C]) for n in ("base", "h1", "gate_r", "norm3"))
        split, split3 = sb("split", [TP, TILES, 2 * C], F32R), sb("split3", [TP, TILES, 2 * C], F32R)
        Small = [tuple(sb(n + i, shape, dt) for n, shape, dt in (
            ("stats", [TP, TILES, 6], F32), ("mv", [TP, TILES, 2], F32), ("var", [TP, 2, TILES], F32),
            ("rstd", [TP, 2, TILES], F32), ("ny", [TP, 2, TILES], F32), ("seed", [TP, 2, TILES], I32))) for i in "ab"]
        stack = [sb(f"stack{i}", [128, 3, N], F32R) for i in range(3)]
        K, V, R = sb("K", [HALF, W2]), sb("V", [HALF, W2]), sb("R", [HALF, W2])
        M = [sb("Mf", [HALF, W2 + 1]), sb("Mb", [HALF, W2 + 1])]
        E1 = [sb("E1f", [HALF, W2]), sb("E1b", [HALF, W2])]
        SB = [sb("SBf", [HALF, W2 + 1]), sb("SBb", [HALF, W2 + 1])]
        SA = [sb("SAf", [HALF, W2 + 1]), sb("SAb", [HALF, W2 + 1])]
        top, own = sb("top", [HALF, W2]), sb("own", [HALF, W2])
        AFTER = (slice(1, W2 + 1), slice(0, W2))
        BEFORE = (slice(0, W2), slice(1, W2 + 1))
        act, hid = sb("act", [128, 2, N]), sb("hid", [128, 2, N])
        sc, sfc, tmp_e, sel_e, eqs = (sb(n, [TP, TILES, EXPERTS]) for n in ("sc", "sfc", "tmp_e", "sel_e", "eqs"))
        pa, pb2, pc, pd = (sb(n, [TP, TILES, EGROUPS]) for n in ("pa", "pb2", "pc", "pd"))
        cmp1, cmp2 = (sb(n, [TP, TILES, EGROUPS, EGROUPS]) for n in ("cmp1", "cmp2"))
        top8 = sb("top8", [TP, TILES, 8])
        cnt = sb("cnt", [TP, TILES])
        c48 = sb("c48", [TP, TILES, CROWS], F32R)
        cT = sb("cT", [CROWS, N], F32R)

        PF = pb("PF", [128, 2, 512])
        PG = pb("PG", [128, 2, 2, 512])
        PA = pb("PA", [128, 2, 512])

        raw_in = [sem(f"raw_in{i}") for i in range(RING)]
        hi_done, lo_done = sem("hi_done"), sem("lo_done")
        consts_in = sem("consts_in")
        consts_done = sem("consts_done")
        setup_v = sem("setup_v")
        whole_in = {name: sem(f"in_{name}") for name, _, _ in WHOLE}
        pat_in = counted("pat_in", 16)
        pe_tok = counted("pe_tok", 1)
        tok_out = counted("tok_out", 2)
        split_ready = counted("split_ready", 2)
        pe_transposed = counted("pe_transposed", 6)
        act_stack = counted("act_stack", 6)
        pe_kvr = counted("pe_kvr", 3)
        act_kvr = counted("act_kvr", 3)
        exp_in = counted("exp_in", 5)
        exp_out = counted("exp_out", 7)
        z_ready = counted("z_ready", 1)
        pe_o = counted("pe_o", 1)
        front_step = counted("front_step", FRONT_STEPS)
        pe_rf = counted("pe_rf", 1)
        act_rf = counted("act_rf", 1)
        pe_up = counted("pe_up", UPS)
        act_relu = counted("act_relu", UPS)
        act_square = counted("act_square", UPS)
        pe_mix = counted("pe_mix", UPS)
        split3_ready = counted("split3_ready", 1)
        pe_transposed3 = counted("pe_transposed3", 3)
        act_stack3 = counted("act_stack3", 3)
        pe_router = counted("pe_router", 1)
        logits_ready = counted("logits_ready", 1)
        act_score = counted("act_score", 1)
        c_ready = counted("c_ready", 1)
        pe_cT = counted("pe_cT", 1)
        act_cT = counted("act_cT", 1)
        pe_gu = counted("pe_gu", SCH + ECH)
        act_silu = counted("act_silu", SCH + ECH)
        hid_ready = counted("hid_ready", SCH + ECH)
        pe_down = counted("pe_down", SCH + ECH)
        out_ready = counted("out_ready", 2, 1)
        out_stored = counted("out_stored", 16 * TILES, 1)
        back_step = counted("back_step", BACK_STEPS)
        block = ctx.enter_context(nc.Block())

        BANKS = ((0, 0, 2), (1, 2, 3))

        def rows(P, bank, a, b):
            return P[0:TP, bank, 0:(b - a) * C].rearrange("p (t c) -> p t c", c=C)

        def tile_out(P, t):
            return P[0:TP, t // 2, (t % 2) * C:(t % 2 + 1) * C]

        def halves(P):
            return P[0:HALF, :, 0:N]

        def two(x):
            return x[:, 0:W2].rearrange("p (h n) -> p h n", h=2)

        @block.sync
        def _(sp):
            def piece(n):
                name, prt, slots, cols, _ = PIECES[n]
                if n >= RING:
                    sp.wait_ge(lo_done, n - RING + 1)
                sp.dma_start(raw[n % RING][0:prt, 0:slots * cols],
                             A[f"w_{name}"]).then_inc(raw_in[n % RING], 16)

            def unsplit(name):
                sp.dma_start(whole[name][:, :, :], A[f"w_{name}"]).then_inc(whole_in[name], 16)

            def patches(g):
                sp.dma_start(pat[:, :, :], A["patches"][bass.ds(g, 1)].rearrange("a p k n -> (a p) k n")).then_inc(pat_in, 16)

            def store(g):
                sp.wait_ge(out_ready, at(out_ready, g, 2))
                for t in range(TILES):
                    skip = TS[t - 1] + TP - TS[t] if t else 0
                    sp.dma_start(A["out"][bass.ds(g, 1), TS[t] + skip:TS[t] + TP, :].rearrange("a p c -> (a p) c"),
                                 h1[skip:TP, t, :]).then_inc(out_stored, 16)

            patches(0)
            unsplit("tok")
            for n in range(3):
                piece(n)
            unsplit("o")
            for n in range(3, 6):
                piece(n)
            unsplit("down")
            sp.wait_ge(pe_tok, at(pe_tok, 0, 1))
            patches(1)
            for n in range(6, 8):
                piece(n)
            unsplit("sd")
            for n in range(8, 11):
                piece(n)
            unsplit("ed")
            for n in range(11, len(PIECES)):
                piece(n)
            with sp.Fori(2, GROUPS) as g:
                sp.wait_ge(pe_tok, at(pe_tok, g - 1, 1))
                patches(g)
                store(g - 2)
            store(GROUPS - 2)
            store(GROUPS - 1)
            sp.wait_ge(out_stored, at(out_stored, GROUPS, 0))

        @block.gpsimd
        def _(pool):
            for n, (name, prt, slots, cols, has_lo) in enumerate(PIECES):
                src = raw[n % RING][0:prt, 0:slots * cols].rearrange("p (s c) -> p s c", s=slots)
                pool.wait_ge(hi_done, n + 1)
                if n:
                    pool.wait_ge(lo_done, n)
                if name == "bd":
                    low = slice(2 * EXPERTS, CROWS)
                    nc.gpsimd.tensor_tensor(hi[name][low, :, :], src[low], hi[name][low, :, :].bitcast(F32),
                                            ALU.subtract).then_inc(lo_done, 1)
                elif not has_lo:
                    nc.gpsimd.memset(nothing[:, n:n + 1], 0.0).then_inc(lo_done, 1)
                else:
                    nc.gpsimd.tensor_tensor(lo[name][:, :, :], src, hi[name][:, :, :].bitcast(F32),
                                            ALU.subtract).then_inc(lo_done, 1)

        def weave(main, side, plan):
            done = 0
            for place in main:
                most, up_to = plan.get(place, (0, 0))
                for _ in range(min(most, up_to - done)):
                    next(side, None)
                    done += 1
            for _ in side:
                pass


        def act_high_parts(act_e):
            for n, (name, prt, slots, cols, _) in enumerate(PIECES):
                act_e.wait_ge(raw_in[n % RING], 16 * (n // RING + 1))
                nc.scalar.activation(hi[name][:, :, :], raw[n % RING][0:prt, 0:slots * cols].rearrange("p (s c) -> p s c", s=slots),
                                     ACT.Copy).then_inc(hi_done, 1)
                yield

        def act_front(act_e, g):
            def stacks(n):
                for k in range(3 * n, 3 * n + 3):
                    act_e.wait_ge(pe_transposed, at(pe_transposed, g, k + 1))
                    nc.scalar.activation(stack[n][:, k % 3, :], PF[:, k % 2, 0:N], ACT.Copy).then_inc(act_stack, 1)
                    yield "stack"

            yield from stacks(0)
            for n, (dst, f, scale) in enumerate(((K, ACT.Copy, 1.0), (V, ACT.Copy, 1.0), (R, ACT.Exp, -1.0))):
                act_e.wait_ge(pe_kvr, at(pe_kvr, g, n + 1))
                nc.scalar.activation(two(dst), halves(PF), f, scale=scale).then_inc(act_kvr, 1)
                yield "kvr"
            steps = [(E1[d][:, :], SB[d][:, AFTER[d]]) for d in range(2)]
            steps += [(M[d][:, BEFORE[d]],) for d in range(2)] + [(own[:, :],)]
            for n, arrays in enumerate(steps):
                act_e.wait_ge(exp_in, at(exp_in, g, n + 1))
                for a in arrays:
                    nc.scalar.activation(a, a, ACT.Exp).then_inc(exp_out, 1)
                yield "exp"
            yield from stacks(1)

        def act_back(act_e, g):
            act_e.wait_ge(pe_rf, at(pe_rf, g, 1))
            for bank, a, b in BANKS:
                last = nc.scalar.activation(gate_r[:, a:b, :], PG[0:TP, bank, 1, 0:(b - a) * C].rearrange("p (t c) -> p t c", c=C),
                                            ACT.Tanh, scale=0.5)
            last.then_inc(act_rf, 1)
            for m in range(UPS):
                i = m % 2
                act_e.wait_ge(pe_up, at(pe_up, g, m + 1))
                if m >= 2:
                    act_e.wait_ge(act_square, at(act_square, g, m - 1))
                nc.scalar.activation(act[:, i, :], PG[:, i, 0, 0:N], ACT.Relu).then_inc(act_relu, 1)
                act_e.wait_ge(act_relu, at(act_relu, g, m + 1))
                if m >= 2:
                    act_e.wait_ge(pe_mix, at(pe_mix, g, m - 1))
                nc.scalar.activation(hid[:, i, :], act[:, i, :], ACT.Square).then_inc(act_square, 1)
                yield f"mix{m}"
            for p in range(3):
                act_e.wait_ge(pe_transposed3, at(pe_transposed3, g, p + 1))
                nc.scalar.activation(stack[2][:, p, :], PG[:, p // 2, p % 2, 0:N], ACT.Copy).then_inc(act_stack3, 1)
            yield "stacked3"
            act_e.wait_ge(logits_ready, at(logits_ready, g, 1))
            nc.scalar.activation(sc[:, :, :], sc[:, :, :], ACT.Tanh, scale=0.5).then_inc(act_score, 1)
            yield "scored"
            act_e.wait_ge(act_square, at(act_square, g, UPS))
            for n in range(SCH + ECH):
                prt, bias = (INNER, sgb[:, n:n + 1]) if n < SCH else (128, egb[:, n - SCH:n - SCH + 1])
                act_e.wait_ge(pe_gu, at(pe_gu, g, n + 1))
                if n >= 2:
                    act_e.wait_ge(hid_ready, at(hid_ready, g, n - 1))
                nc.scalar.activation(act[0:prt, n % 2, :], PG[0:prt, n % 2, 0, 0:N], ACT.Silu, bias=bias).then_inc(act_silu, 1)
                if n == SCH - 1:
                    act_e.wait_ge(pe_cT, at(pe_cT, g, 1))
                    nc.scalar.activation(cT[:, :], PA[0:CROWS, 1, C:C + N], ACT.Copy).then_inc(act_cT, 1)
                yield f"silu{n}"

        @block.scalar
        def _(act_e):
            loads = [(ident32[:, :], A["ident"])]
            for dst, src in ((ln1w, "ln1_w"), (ln1b, "ln1_b"), (ln2w, "ln2_w"), (ln2b, "ln2_b"), (sbd, "sbd")):
                loads.append((dst[:, :], A[src].broadcast_to([TP, C])))
            loads += [(rbias[:, :], A["router_b"].broadcast_to([TP, EXPERTS])),
                      (cbias[:, :], A["corr_bias"].broadcast_to([TP, EXPERTS])),
                      (before[:, :, :].rearrange("p i j -> p (i j)"), A["before"].broadcast_to([TP, EGROUPS * EGROUPS])),
                      (decay[:, :], A["decay"]), (first[:, :], A["first"]),
                      (egb[:, :], A["egb"]), (eub[:, :], A["eub"]), (sgb[:, :], A["sgb"]), (sub_[:, :], A["sub"])]
            assert len(loads) == N_CONST_LOADS
            for dst, src in loads:
                act_e.dma_start(dst, src).then_inc(consts_in, 16)
            act_e.wait_ge(consts_done, 1)
            for b in range(IMGS):
                for t in range(TILES):
                    if 0 <= b * T - TS[t] < TP:
                        act_e.dma_start(cls_rows[b * T - TS[t]:b * T - TS[t] + 1, t, :], A["cls"]).then_inc(consts_in, 16)
            high = act_high_parts(act_e)
            for _ in range(3):
                next(high)
            weave(act_front(act_e, 0), high, {"stack": (1, 99), "kvr": (2, 99), "exp": (2, 99)})
            with act_e.Fori(0, GROUPS - 1) as g:
                weave(act_back(act_e, g), act_front(act_e, g + 1), PLAN["act"])
            for _ in act_back(act_e, GROUPS - 1):
                pass

        V_ = nc.vector

        def stepper(v, g, sem, spare):
            count, spares = [0], [0]

            def step(ins):
                count[0] += 1
                ins.then_inc(sem, 1)

            def settle():
                v.wait_ge(sem, at(sem, g, count[0]))

            def do(ins):
                step(ins)
                settle()

            def settle_apart():
                settle()
                V_.memset(spare[:, spares[0]:spares[0] + 1], 0.0)
                spares[0] += 1

            return step, settle, do, settle_apart, count

        def moments(steps, small, x):
            step, settle, do, settle_apart, _ = steps
            stats, mv, var = small[0:3]
            for t in range(TILES):
                step(V_.bn_stats(stats[:, t, :], x[:, t, :]))
            settle_apart()
            for t in range(TILES):
                step(V_.bn_aggr(mv[:, t, :], stats[:, t, :]))
            settle()
            yield
            do(V_.tensor_scalar(var[:, 0, :], mv[:, :, 1], EPS, None, ALU.add))
            yield

        def rsqrt(steps, small, cols):
            _, _, do, _, _ = steps
            var, rstd, ny, seed = (x[:, 0:cols, :] for x in small[2:6])
            do(V_.tensor_scalar(seed, var.bitcast(I32), 1, None, ALU.logical_shift_right))
            yield
            do(V_.tensor_scalar(rstd.bitcast(I32), seed, -1.0, RSQRT_SEED, ALU.mult, ALU.add))
            for _ in range(3):
                yield
                do(V_.tensor_tensor(ny, rstd, rstd, ALU.mult))
                yield
                do(V_.scalar_tensor_tensor(ny, ny, -0.5, var, ALU.mult, ALU.mult))
                yield
                do(V_.scalar_tensor_tensor(rstd, ny, 1.5, rstd, ALU.add, ALU.mult))
            yield

        def normalise(steps, small, dst, x):
            step, settle, _, _, _ = steps
            for t in range(TILES):
                step(V_.tensor_scalar(dst[:, t, :], x[:, t, :], small[1][:, t, 0:1], small[3][:, 0, t:t + 1],
                                      ALU.subtract, ALU.mult))
            settle()
            yield

        def affine(steps, x, w, b):
            _, _, do, _, _ = steps
            do(V_.tensor_tensor(x[:, :, :], x[:, :, :], w[:, None, :].broadcast_to([TP, TILES, C]), ALU.mult))
            yield
            do(V_.tensor_tensor(x[:, :, :], x[:, :, :], b[:, None, :].broadcast_to([TP, TILES, C]), ALU.add))
            yield

        def split_rows(steps, dst, x, ready):
            step, settle, do, _, _ = steps
            do(V_.tensor_copy(dst[:, :, 0:C], x[:, :, :]))
            yield
            do(V_.tensor_tensor(dst[:, :, C:256], x[:, :, 128:C], dst[:, :, 128:C].bitcast(F32), ALU.subtract))
            V_.tensor_tensor(dst[:, :, 256:384], x[:, :, 0:128], dst[:, :, 0:128].bitcast(F32),
                             ALU.subtract).then_inc(ready, 1)
            yield

        def dve_front(v, g):
            steps = stepper(v, g, front_step, spare_v[:, 0:4])
            step, settle, do, settle_apart, count = steps
            small = Small[0]
            _, mv, var, rstd, _, _ = small
            v.wait_ge(pe_tok, at(pe_tok, g, 1))
            for bank, a, b in BANKS:
                V_.tensor_tensor(h0[:, a:b, :], rows(PF, bank, a, b), cls_rows[:, a:b, :], ALU.add).then_inc(tok_out, 1)
            v.wait_ge(tok_out, at(tok_out, g, 2))
            yield
            yield from moments(steps, small, h0)
            do(V_.reciprocal(var[:, 1, :], var[:, 0, :]))
            yield
            do(V_.tensor_tensor(var[:, 1, :], var[:, 1, :], mv[:, :, 1], ALU.mult))
            yield
            do(V_.tensor_scalar(var[:, 1, :], var[:, 1, :], EPS, None, ALU.add))
            yield from rsqrt(steps, small, 2)
            yield from normalise(steps, small, x0, h0)
            for t in range(TILES):
                step(V_.tensor_scalar(norm[:, t, :], x0[:, t, :], rstd[:, 1, t:t + 1], None, ALU.mult))
            settle()
            yield
            yield from affine(steps, norm, ln1w, ln1b)
            yield from split_rows(steps, split, norm, split_ready)
            v.wait_ge(split_ready, at(split_ready, g, 1))

            def run(x, d):
                return x if d == 0 else x[:, ::-1]

            v.wait_ge(act_kvr, at(act_kvr, g, 1))
            for d, dec in enumerate((dec_f, dec_b)):
                do(V_.tensor_tensor_scan(run(M[d][:, AFTER[d]], d), run(dec[:, :], d), run(K[:, :], d), 0.0, ALU.add, ALU.max))
                yield
            for d in range(2):
                old, new = M[d][:, BEFORE[d]], M[d][:, AFTER[d]]
                for h in range(2):
                    s = slice(h * N, (h + 1) * N)
                    step(V_.scalar_tensor_tensor(E1[d][:, s], old[:, s], decay[:, h:h + 1], new[:, s], ALU.add, ALU.subtract))
                    yield
                do(V_.tensor_tensor(SB[d][:, AFTER[d]], K[:, :], new, ALU.subtract))
                start = 0 if d == 0 else T - 1
                do(V_.memset(old[:, start::T], NEG))
                V_.memset(E1[d][:, start::T], NEG).then_inc(exp_in, 1)
                yield
            mf, mb = M[0][:, BEFORE[0]], M[1][:, BEFORE[1]]
            do(V_.tensor_tensor(top[:, :], mf, mb, ALU.max))
            yield
            for h in range(2):
                s = slice(h * N, (h + 1) * N)
                step(V_.scalar_tensor_tensor(top[:, s], K[:, s], first[:, h:h + 1], top[:, s], ALU.add, ALU.max))
            settle()
            yield
            V_.tensor_tensor(mf, mf, top[:, :], ALU.subtract).then_inc(exp_in, 1)
            yield
            V_.tensor_tensor(mb, mb, top[:, :], ALU.subtract).then_inc(exp_in, 1)
            yield
            do(V_.scalar_tensor_tensor(own[:, 0:N], K[:, 0:N], first[:, 0:1], top[:, 0:N], ALU.add, ALU.subtract))
            V_.scalar_tensor_tensor(own[:, N:W2], K[:, N:W2], first[:, 1:2], top[:, N:W2], ALU.add, ALU.subtract).then_inc(exp_in, 1)
            yield
            v.wait_ge(act_kvr, at(act_kvr, g, 2))
            for d in range(2):
                v.wait_ge(exp_out, at(exp_out, g, 2 * d + 2))
                a, b = SA[d][:, AFTER[d]], SB[d][:, AFTER[d]]
                do(V_.tensor_tensor(a, b, V[:, :], ALU.mult))
                yield
                step(V_.tensor_tensor_scan(run(a, d), run(E1[d][:, :], d), run(a, d), 0.0, ALU.mult, ALU.add))
                yield
                do(V_.tensor_tensor_scan(run(b, d), run(E1[d][:, :], d), run(b, d), 0.0, ALU.mult, ALU.add))
                yield
            for d in range(2):
                v.wait_ge(exp_out, at(exp_out, g, 5 + d))
                for x in (SA[d], SB[d]):
                    step(V_.tensor_tensor(x[:, BEFORE[d]], x[:, BEFORE[d]], M[d][:, BEFORE[d]], ALU.mult))
                    yield
            v.wait_ge(exp_out, at(exp_out, g, 7))
            do(V_.tensor_tensor(V[:, :], V[:, :], own[:, :], ALU.mult))
            yield
            step(V_.tensor_tensor(top[:, :], SA[0][:, BEFORE[0]], SA[1][:, BEFORE[1]], ALU.add))
            yield
            do(V_.tensor_tensor(K[:, :], SB[0][:, BEFORE[0]], SB[1][:, BEFORE[1]], ALU.add))
            yield
            step(V_.tensor_tensor(top[:, :], top[:, :], V[:, :], ALU.add))
            yield
            do(V_.tensor_tensor(K[:, :], K[:, :], own[:, :], ALU.add))
            yield
            v.wait_ge(act_kvr, at(act_kvr, g, 3))
            do(V_.scalar_tensor_tensor(K[:, :], R[:, :], 1.0, K[:, :], ALU.add, ALU.mult))
            yield
            for h in range(2):
                s = slice(h * N, (h + 1) * N)
                step(V_.reciprocal(K[:, s], K[:, s]))
                yield
            settle()
            V_.tensor_tensor(K[:, :], K[:, :], top[:, :], ALU.mult).then_inc(z_ready, 1)
            yield

            v.wait_ge(pe_o, at(pe_o, g, 1))
            for bank, a, b in BANKS:
                step(V_.tensor_tensor(x0[:, a:b, :], x0[:, a:b, :], rows(PF, bank, a, b), ALU.add))
            settle()
            yield
            yield from moments(steps, small, x0)
            yield from rsqrt(steps, small, 1)
            yield from normalise(steps, small, norm, x0)
            yield from affine(steps, norm, ln2w, ln2b)
            v.wait_ge(pe_transposed, at(pe_transposed, g, 3))
            yield from split_rows(steps, split, norm, split_ready)
            v.wait_ge(split_ready, at(split_ready, g, 2))
            do(V_.tensor_tensor(base[:, :, :], h0[:, :, :], x0[:, :, :], ALU.add))
            assert count[0] == per_group[front_step], count
            yield

        def dve_back(v, g):
            steps = stepper(v, g, back_step, spare_v[:, 4:8])
            step, settle, do, settle_apart, count = steps
            small = Small[1]
            yield "mix"
            v.wait_ge(act_rf, at(act_rf, g, 1))
            v.wait_ge(pe_mix, at(pe_mix, g, UPS))
            v.wait_ge(out_stored, at(out_stored, g, 0))
            for bank, a, b in BANKS:
                step(V_.scalar_tensor_tensor(gate_r[:, a:b, :], gate_r[:, a:b, :], 1.0, rows(PA, bank, a, b), ALU.add, ALU.mult))
            settle()
            yield "LN3"
            do(V_.scalar_tensor_tensor(h1[:, :, :], gate_r[:, :, :], 0.5, base[:, :, :], ALU.mult, ALU.add))
            yield "LN3"
            for _ in moments(steps, small, h1):
                yield "LN3"
            for _ in rsqrt(steps, small, 1):
                yield "LN3"
            for _ in normalise(steps, small, norm3, h1):
                yield "LN3"
            for _ in split_rows(steps, split3, norm3, split3_ready):
                yield "LN3"
            do(V_.tensor_tensor(h1[:, :, :], h1[:, :, :], sbd[:, None, :].broadcast_to([TP, TILES, C]), ALU.add))
            yield "router"
            v.wait_ge(pe_router, at(pe_router, g, 1))
            E3 = [TP, TILES, EXPERTS]
            V_.tensor_tensor(sc[:, :, :], PA[0:TP, 0, 0:TILES * EXPERTS].rearrange("p (t e) -> p t e", e=EXPERTS),
                             rbias[:, None, :].broadcast_to(E3), ALU.add).then_inc(logits_ready, 1)
            yield "score"
            v.wait_ge(act_score, at(act_score, g, 1))
            do(V_.tensor_scalar(sc[:, :, :], sc[:, :, :], 1.0, 0.5, ALU.add, ALU.mult))
            do(V_.tensor_tensor(sfc[:, :, :], sc[:, :, :], cbias[:, None, :].broadcast_to(E3), ALU.add))
            yield "router"
            quad = sfc[:, :, :].rearrange("p t (g e) -> p t g e", e=EPG)
            q = [quad[:, :, :, i] for i in range(EPG)]
            P_, S_ = tmp_e[:, :, 0:EGROUPS], tmp_e[:, :, EGROUPS:2 * EGROUPS]
            step(V_.tensor_tensor(pa[:, :, :], q[0], q[1], ALU.max))
            step(V_.tensor_tensor(pb2[:, :, :], q[0], q[1], ALU.min))
            step(V_.tensor_tensor(pc[:, :, :], q[2], q[3], ALU.max))
            step(V_.tensor_tensor(pd[:, :, :], q[2], q[3], ALU.min))
            settle()
            step(V_.tensor_tensor(P_, pa[:, :, :], pc[:, :, :], ALU.max))
            step(V_.tensor_tensor(S_, pa[:, :, :], pc[:, :, :], ALU.min))
            do(V_.tensor_tensor(pb2[:, :, :], pb2[:, :, :], pd[:, :, :], ALU.max))
            do(V_.tensor_tensor(S_, S_, pb2[:, :, :], ALU.max))
            yield "router"
            do(V_.tensor_tensor(pa[:, :, :], P_, S_, ALU.add))
            yield "router"
            G4 = [TP, TILES, EGROUPS, EGROUPS]
            other, mine = pa[:, :, None, :].broadcast_to(G4), pa[:, :, :, None].broadcast_to(G4)
            step(V_.tensor_tensor(cmp1[:, :, :, :], other, mine, ALU.is_gt))
            do(V_.tensor_tensor(cmp2[:, :, :, :], other, mine, ALU.is_equal))
            yield "router"
            do(V_.tensor_tensor(cmp2[:, :, :, :], cmp2[:, :, :, :], before[:, None, :, :].broadcast_to(G4), ALU.mult))
            yield "router"
            do(V_.tensor_tensor(cmp1[:, :, :, :], cmp1[:, :, :, :], cmp2[:, :, :, :], ALU.add))
            yield "router"
            do(V_.tensor_reduce(pa[:, :, :], cmp1[:, :, :, :], AXX, ALU.add))
            yield "router"
            do(V_.tensor_scalar(pa[:, :, :], pa[:, :, :], float(TOPG), None, ALU.is_lt))
            yield "router"
            step(V_.tensor_tensor(quad, quad, pa[:, :, :, None].broadcast_to([TP, TILES, EGROUPS, EPG]), ALU.mult))
            settle_apart()
            for t in range(TILES):
                step(V_.max(top8[:, t, :], sfc[:, t, :]))
            settle()
            yield "router"
            fourth = top8[:, :, TOPK - 1:TOPK].broadcast_to(E3)
            step(V_.tensor_tensor(sel_e[:, :, :], sfc[:, :, :], fourth, ALU.is_gt))
            do(V_.tensor_tensor(eqs[:, :, :], sfc[:, :, :], fourth, ALU.is_equal))
            yield "router"
            do(V_.tensor_reduce(cnt[:, :], sel_e[:, :, :], AXX, ALU.add))
            yield "router"
            for t in range(TILES):
                step(V_.tensor_tensor_scan(tmp_e[:, t, :], ones_e[:, :], eqs[:, t, :], cnt[:, t:t + 1], ALU.mult, ALU.add))
            settle()
            yield "router"
            do(V_.scalar_tensor_tensor(tmp_e[:, :, :], tmp_e[:, :, :], float(TOPK), eqs[:, :, :], ALU.is_le, ALU.mult))
            yield "router"
            do(V_.tensor_tensor(sel_e[:, :, :], sel_e[:, :, :], tmp_e[:, :, :], ALU.add))
            yield "router"
            do(V_.tensor_tensor(sc[:, :, :], sc[:, :, :], sel_e[:, :, :], ALU.mult))
            yield "router"
            do(V_.tensor_reduce(cnt[:, :], sc[:, :, :], AXX, ALU.add))
            yield "router"
            do(V_.tensor_scalar(cnt[:, :], cnt[:, :], 1e-20, None, ALU.add))
            do(V_.reciprocal(cnt[:, :], cnt[:, :]))
            yield "router"
            do(V_.scalar_tensor_tensor(sc[:, :, :], sc[:, :, :], SCALE, cnt[:, :, None].broadcast_to(E3), ALU.mult, ALU.mult))
            yield "router"
            step(V_.tensor_copy(c48[:, :, 0:EXPERTS], sc[:, :, :]))
            do(V_.tensor_copy(c48[:, :, 2 * EXPERTS:3 * EXPERTS], sc[:, :, :]))
            V_.tensor_tensor(c48[:, :, EXPERTS:2 * EXPERTS], sc[:, :, :], c48[:, :, 0:EXPERTS].bitcast(F32),
                             ALU.subtract).then_inc(c_ready, 1)
            yield "routed"

            for n in range(SCH + ECH):
                i, prt = n % 2, INNER if n < SCH else 128
                v.wait_ge(act_silu, at(act_silu, g, n + 1))
                if n < SCH:
                    bias = sub_[:, n:n + 1]
                else:
                    bias = eub[:, n - SCH:n - SCH + 1]
                    gates = act[:, i, :].rearrange("p (h n) -> p h n", h=2)
                    do(V_.tensor_tensor(gates, gates, PG[:, i, :, N:N + N // 2], ALU.mult))
                if n >= 2:
                    v.wait_ge(pe_down, at(pe_down, g, n - 1))
                V_.scalar_tensor_tensor(hid[0:prt, i, :], PG[0:prt, i, 1, 0:N], bias, act[0:prt, i, :],
                                        ALU.add, ALU.mult).then_inc(hid_ready, 1)
                yield f"hid{n}"
            v.wait_ge(pe_down, at(pe_down, g, SCH + ECH))
            for bank, a, b in BANKS:
                V_.tensor_tensor(h1[:, a:b, :], h1[:, a:b, :], rows(PA, bank, a, b), ALU.add).then_inc(out_ready, 1)
            assert count[0] == per_group[back_step], count
            yield "out"

        @block.vector
        def _(v):
            count = [0]

            def setup(ins):
                count[0] += 1
                ins.then_inc(setup_v, 1)

            nc.vector.memset(cls_rows[:, :, :], 0.0).then_inc(consts_done, 1)
            for d in range(2):
                edge = 0 if d == 0 else W2
                for a in (M[d], SA[d], SB[d]):
                    setup(nc.vector.memset(a[:, edge:edge + 1], 0.0))
            nc.vector.memset(spare_v[:, 2:3], 0.0).then_inc(out_ready, 1)
            nc.vector.memset(spare_v[:, 3:4], 0.0).then_inc(out_stored, 1)
            setup(nc.vector.memset(own[:, :], 0.0))
            setup(nc.vector.memset(ones_e[:, :], 1.0))
            v.wait_ge(consts_in, 16 * (N_CONST_LOADS + N_CLS))
            setup(nc.vector.tensor_copy(ident[:, :], ident32[:, :]))
            setup(nc.vector.tensor_scalar(decay[:, :], decay[:, :], 1.0 / T, None, ALU.mult))
            setup(nc.vector.tensor_scalar(first[:, :], first[:, :], 1.0 / T, None, ALU.mult))
            v.wait_ge(setup_v, count[0])
            for a in (dec_f, dec_b):
                for h in range(2):
                    setup(nc.vector.tensor_scalar(a[:, h * N:(h + 1) * N], own[:, 0:N], decay[:, h:h + 1], None, ALU.add))
            v.wait_ge(setup_v, count[0])
            setup(nc.vector.memset(dec_f[:, 0:W2:T], NEG))
            nc.vector.memset(dec_b[:, T - 1:W2:T], NEG).then_inc(consts_done, 1)
            v.wait_ge(setup_v, count[0])
            v.wait_ge(consts_done, 2)
            for _ in dve_front(v, 0):
                pass
            with v.Fori(0, GROUPS - 1) as g:
                weave(dve_back(v, g), dve_front(v, g + 1), PLAN["dve"])
            for _ in dve_back(v, GROUPS - 1):
                pass

        mm = nc.tensor.matmul

        def need(pe, name):
            pe.wait_ge(lo_done, PIECE_AT[name] + 1)

        def from_stack(out, x, name, cols):
            w_hi, w_lo = hi[name], lo[name]
            for p, slot in enumerate((0, 1, 0)):
                mm(out, w_hi[:, slot, cols], x[:, p, :], start=(p == 0), stop=False)
            for p in range(2):
                last = mm(out, w_lo[:, p, cols], x[:, p, :], start=False, stop=(p == 1))
            return last

        def rows_from_stack(out, opens, x, name, cols):
            w_hi, w_lo = hi[name], lo[name]
            for t in range(TILES):
                for p, slot in enumerate((0, 1, 0)):
                    mm(out(t), x[:, p, TS[t]:TS[t] + TP], w_hi[:, slot, cols],
                       start=(p == 0 and t in opens), stop=False, skip_group_check=True)
                for p in range(2):
                    last = mm(out(t), x[:, p, TS[t]:TS[t] + TP], w_lo[:, p, cols],
                              start=False, stop=(p == 1), skip_group_check=True)
            return last

        def down(P, src, w, start, stop):
            for t in range(TILES):
                last = mm(tile_out(P, t), src[:, TS[t]:TS[t] + TP], w, start=start and t != 1, stop=stop, skip_group_check=True)
            return last

        def pe_front(pe, g, first_group=False):
            if not first_group:
                pe.wait_ge(act_stack, at(act_stack, g, 0))
            pe.wait_ge(whole_in["tok"], 16)
            pe.wait_ge(pat_in, at(pat_in, g, 16))
            for k in range(2):
                last = down(PF, pat[:, k, :], whole["tok"][:, k, :], k == 0, k == 1)
            last.then_inc(pe_tok, 1)
            yield

            def transposes(n):
                pe.wait_ge(split_ready, at(split_ready, g, n + 1))
                for p in range(3):
                    k = 3 * n + p
                    if p == 2:
                        pe.wait_ge(act_stack, at(act_stack, g, k - 1))
                    for t in range(TILES):
                        last = nc.tensor.transpose(PF[:, k % 2, TS[t]:TS[t] + TP].bitcast(F32R),
                                                   split[:, t, p * 128:(p + 1) * 128], ident[0:TP, 0:TP])
                    last.then_inc(pe_transposed, 1)

            transposes(0)
            yield
            for n, name in enumerate(("k", "v", "r")):
                need(pe, name)
                if n == 0:
                    pe.wait_ge(act_stack, at(act_stack, g, 3))
                else:
                    pe.wait_ge(act_kvr, at(act_kvr, g, n))
                for h in range(2):
                    last = from_stack(PF[0:HALF, h, 0:N], stack[0], name, slice(h * HALF, (h + 1) * HALF))
                last.then_inc(pe_kvr, 1)
                yield
            pe.wait_ge(whole_in["o"], 16)
            pe.wait_ge(z_ready, at(z_ready, g, 1))
            for h in range(2):
                last = down(PF, K[:, h * N:(h + 1) * N], whole["o"][:, h, :], h == 0, h == 1)
            last.then_inc(pe_o, 1)
            yield
            transposes(1)
            yield

        def pe_back(pe, g):
            yield "start"
            pe.wait_ge(act_stack, at(act_stack, g, 6))
            need(pe, "rf")
            rows_from_stack(lambda t: PG[0:TP, t // 2, 1, (t % 2) * C:(t % 2 + 1) * C], (0, 2), stack[1],
                            "rf", slice(0, C)).then_inc(pe_rf, 1)

            def up(m):
                need(pe, f"up{m // 3}")
                if m >= 2:
                    pe.wait_ge(act_relu, at(act_relu, g, m - 1))
                from_stack(PG[:, m % 2, 0, 0:N], stack[1], f"up{m // 3}", slice(m % 3 * 128, (m % 3 + 1) * 128)).then_inc(pe_up, 1)

            up(0)
            pe.wait_ge(whole_in["down"], 16)
            for m in range(UPS):
                if m + 1 < UPS:
                    up(m + 1)
                if m == 0:
                    pe.wait_ge(out_ready, at(out_ready, g, 0))
                pe.wait_ge(act_square, at(act_square, g, m + 1))
                down(PA, hid[:, m % 2, :], whole["down"][:, m, :], m == 0, m == UPS - 1).then_inc(pe_mix, 1)
                yield f"mix{m}"
            pe.wait_ge(split3_ready, at(split3_ready, g, 1))
            for p in range(3):
                for t in range(TILES):
                    last = nc.tensor.transpose(PG[:, p // 2, p % 2, TS[t]:TS[t] + TP].bitcast(F32R),
                                               split3[:, t, p * 128:(p + 1) * 128], ident[0:TP, 0:TP])
                last.then_inc(pe_transposed3, 1)
            pe.wait_ge(act_stack3, at(act_stack3, g, 3))
            need(pe, "router")
            rows_from_stack(lambda t: PA[0:TP, 0, t * EXPERTS:(t + 1) * EXPERTS], (0,), stack[2],
                            "router", slice(0, EXPERTS)).then_inc(pe_router, 1)
            yield "router"

            def gate_up(n):
                i = n % 2
                if n >= 2:
                    pe.wait_ge(hid_ready, at(hid_ready, g, n - 1))
                if n < SCH:
                    name, first_col, width = "sgu", n * 2 * INNER, INNER
                    need(pe, name)
                else:
                    j = n - SCH
                    name, first_col, width = f"egu{j // 2}", (j % 2) * 256, 128
                    need(pe, name)
                    for u in range(2):
                        mm(PG[:, i, u, N:N + N // 2], hi[f"sel{j // 6}"][:, j % 6, :],
                           cT[:, u * (N // 2):(u + 1) * (N // 2)], start=True, stop=True)
                for u in range(2):
                    last = from_stack(PG[0:width, i, u, 0:N], stack[2], name, slice(first_col + u * width, first_col + (u + 1) * width))
                last.then_inc(pe_gu, 1)

            def expert_down(n):
                w = whole["sd"][:, n, :] if n < SCH else whole["ed"][:, n - SCH, :]
                pe.wait_ge(hid_ready, at(hid_ready, g, n + 1))
                down(PA, hid[0:(INNER if n < SCH else 128), n % 2, :], w, n == 0, n == SCH + ECH - 1).then_inc(pe_down, 1)

            gate_up(0)
            gate_up(1)
            pe.wait_ge(whole_in["sd"], 16)
            pe.wait_ge(logits_ready, at(logits_ready, g, 1))
            expert_down(0)
            pe.wait_ge(c_ready, at(c_ready, g, 1))
            for t in range(TILES):
                skip = TS[t - 1] + TP - TS[t] if t else 0
                last = mm(PA[0:CROWS, 1, C + TS[t] + skip:C + TS[t] + TP], c48[:, t, :], ident[0:TP, skip:TP],
                          start=False, stop=True, skip_group_check=True)
            last.then_inc(pe_cT, 1)
            pe.wait_ge(act_cT, at(act_cT, g, 1))
            need(pe, "sel1")
            pe.wait_ge(whole_in["ed"], 16)
            for n in range(2, SCH + ECH):
                gate_up(n)
                if n == 2:
                    for t in range(TILES):
                        mm(tile_out(PA, t), cT[:, TS[t]:TS[t] + TP], hi["bd"][:, 0, :],
                           start=False, stop=False, skip_group_check=True)
                expert_down(n - 1)
                yield f"down{n - 1}"
            expert_down(SCH + ECH - 1)
            yield "end"

        @block.tensor
        def _(pe):
            pe.wait_ge(consts_done, 2)
            for _ in pe_front(pe, 0, True):
                pass
            with pe.Fori(0, GROUPS - 1) as g:
                weave(pe_back(pe, g), pe_front(pe, g + 1), PLAN["pe"])
            for _ in pe_back(pe, GROUPS - 1):
                pass


N_CONST_LOADS = 15
N_CLS = sum(0 <= b * T - t < TP for b in range(IMGS) for t in TS)
FRONT_STEPS, BACK_STEPS = 91, 75
PLAN = {
    "pe": {"start": (1, 1), "mix5": (4, 5), "down1": (1, 6), "down13": (1, 7)},
    "act": {"mix5": (11, 11), "silu15": (3, 14)},
    "dve": {"mix": (22, 22), "LN3": (1, 54), "score": (1, 54), "router": (1, 54), "routed": (54, 54),
            **{f"hid{n}": (2, 74) for n in range(2, SCH + ECH)}},
}


def _stack(w):
    import numpy as np
    wt = w.T
    return np.stack([wt[0:128], np.concatenate([wt[128:192]] * 2)], axis=1)


def kernel(**inputs):
    import numpy as np
    import concourse.bacc as bacc
    from concourse.bass_utils import run_bass_kernel_spmd

    I = {k: np.asarray(v) for k, v in inputs.items()}
    a = {}
    x = I["x"].reshape(GROUPS, IMGS, SIDE, PATCH, SIDE, PATCH).transpose(0, 3, 5, 1, 2, 4)
    pat = np.zeros((GROUPS, PIX, IMGS, T), np.float32)
    pat[..., 1:] = x.reshape(GROUPS, PIX, IMGS, SIDE * SIDE)
    a["patches"] = pat.reshape(GROUPS, 2, 128, N).transpose(0, 2, 1, 3)
    a["cls"] = I["cls_tok"].reshape(1, C)
    a["ident"] = np.eye(128, dtype=np.float32)
    p = np.arange(ECH * 128) // INNER
    sel = np.concatenate([(p == np.arange(EXPERTS)[:, None])] * 2 + [np.zeros((EXPERTS, ECH * 128), bool)]).astype(np.float32)
    a["w_sel0"], a["w_sel1"] = sel[:, :ECH * 64], sel[:, ECH * 64:]
    a["before"] = (np.arange(EGROUPS)[None, :] < np.arange(EGROUPS)[:, None]).astype(np.float32).reshape(1, -1)
    for n in ("ln1_w", "ln1_b", "ln2_w", "ln2_b"):
        a[n] = I["L0_attn_" + n].reshape(1, C)
    for n in ("router_b", "corr_bias", "sbd"):
        a[n] = I["L0_ffn_" + n].reshape(1, -1)
    for n in ("decay", "first"):
        a[n] = I["L0_attn_" + n].reshape(2, HALF).T
    a["egb"], a["eub"] = (I["L0_ffn_" + n].reshape(ECH, 128).T for n in ("gbg", "gbu"))
    a["sgb"], a["sub"] = (I["L0_ffn_" + n].reshape(SCH, INNER).T for n in ("sbg", "sbu"))
    a["w_tok"] = I["L0_tok_W"].T.reshape(2, 128, C).transpose(1, 0, 2)
    for n in ("k", "v", "r"):
        a[f"w_{n}"] = _stack(I[f"L0_attn_W{n}_a"])
    a["w_o"] = I["L0_attn_Wo_a"].T.reshape(2, HALF, C).transpose(1, 0, 2)
    up = _stack(I["L0_attn_Wk_f"])
    a["w_up0"], a["w_up1"] = up[:, :, :HID // 2], up[:, :, HID // 2:]
    a["w_rf"] = _stack(I["L0_attn_Wr_f"])
    a["w_down"] = I["L0_attn_Wv_f"].T.reshape(UPS, 128, C).transpose(1, 0, 2)
    a["w_router"] = _stack(I["L0_ffn_router_w"])
    sg, su = _stack(I["L0_ffn_sWg"].T), _stack(I["L0_ffn_sWu"].T)
    a["w_sgu"] = np.stack([sg.reshape(128, 2, SCH, INNER), su.reshape(128, 2, SCH, INNER)], axis=3)
    a["w_sd"] = I["L0_ffn_sWd"].reshape(SCH, INNER, C).transpose(1, 0, 2)
    a["w_bd"] = np.concatenate([I["L0_ffn_gbd"]] * 3)
    eg, eu = (_stack(I["L0_ffn_" + n].transpose(0, 2, 1).reshape(EXPERTS * INNER, C)) for n in ("gWg", "gWu"))
    egu = np.stack([eg.reshape(128, 2, ECH // 2, 2, 128), eu.reshape(128, 2, ECH // 2, 2, 128)], axis=4)
    a["w_ed"] = I["L0_ffn_gWd"].reshape(ECH, 128, C).transpose(1, 0, 2)
    for i in range(ECH // 2):
        a[f"w_egu{i}"] = egu[:, :, i]
    for name, prt, slots, cols, _ in PIECES:
        a[f"w_{name}"] = a[f"w_{name}"].reshape(prt, slots * cols)

    nc = bacc.Bacc("TRN2", target_bir_lowering=False, num_devices=1, dynamic_dma_scratch_size=1024)
    arrays = {f"in_{k}": np.ascontiguousarray(x) for k, x in a.items()}
    A = {k: nc.dram_tensor(f"in_{k}", arrays[f"in_{k}"].shape, F32, kind="ExternalInput").ap() for k in a}
    A["out"] = nc.dram_tensor("out", (GROUPS, N, C), F32, kind="ExternalOutput").ap()
    build(nc, A)
    r = run_bass_kernel_spmd(nc, [arrays], core_ids=[0])
    return r.results[0]["out"].reshape(BATCH, T, C)
```

```python
from contextlib import ExitStack

import concourse.bass as bass
from concourse import mybir

F32, F32R, I32 = mybir.dt.float32, mybir.dt.float32r, mybir.dt.int32
ALU, ACT = mybir.AluOpType, mybir.ActivationFunctionType
AXX = mybir.AxisListType.X

BATCH, SIDE, PATCH, C = 32, 6, 16, 192
T = SIDE * SIDE + 1
PIX = PATCH * PATCH
GROUPS = 4
IMGS = BATCH // GROUPS
N = IMGS * T
TILES = 3
TP = -(-N // TILES // 2) * 2
TS = [0, (N - TP) // 4 * 2, N - TP]
HID = 4 * C
UPS = HID // 128
EXPERTS, INNER, EGROUPS, TOPG, TOPK = 16, 96, 4, 2, 4
EPG = EXPERTS // EGROUPS
ECH = EXPERTS * INNER // 128
SCH = 2
SCALE = 2.5
EPS = 1e-5
NEG = -1e38
CROWS = 65
CLS = 33
RSQRT_SEED = float(0x5F3759DF)
NB = N // 2
WK = N + NB
BLOCKS = (slice(0, N), slice(N, WK))

def _pieces():
    yield ("cls", CLS, 1, C, False)
    yield ("mask", CLS, 1, N, False)
    yield from ((m, 128, 2, 128 + 3 * 64, True) for m in ("k", "v", "r"))
    yield ("rf", 128, 2, C, True)
    yield from ((f"up{i}", 128, 2, HID // 2, True) for i in range(2))
    yield ("router", 128, 2, EXPERTS, True)
    yield ("sgu", 128, 2, 2 * C, True)
    yield ("bd", CROWS, 1, C, False)
    yield from ((f"sel{i}", CROWS, ECH // 2, 128, False) for i in range(2))
    yield from ((f"egu{i}", 128, 2, 512, True) for i in range(ECH // 2))


WHOLE = [("tok", 128, 2), ("o", 128, 2), ("down", 128, UPS), ("sd", INNER, SCH), ("ed", 128, ECH)]
PIECES = list(_pieces())
PIECE_AT = {p[0]: n for n, p in enumerate(PIECES)}
RING, RING_COLS = 4, 2 * 512


def build(nc, A):
    ctx = ExitStack()
    with ctx:
        def sb(name, shape, dt=F32):
            return ctx.enter_context(nc.sbuf_tensor(name, shape, dt))

        def pb(name, shape):
            return ctx.enter_context(nc.psum_tensor(name, shape, F32))

        def sem(name):
            return ctx.enter_context(nc.semaphore(name))

        per_group, raised_before = {}, {}

        def counted(name, n, before_first=0):
            s = sem(name)
            per_group[s] = n
            raised_before[s] = before_first
            return s

        def at(s, g, n):
            return g * per_group[s] + (raised_before[s] + n)

        hi = {p[0]: sb(f"hi_{p[0]}", [p[1], p[2], p[3]], F32R) for p in PIECES}
        lo = {p[0]: sb(f"lo_{p[0]}", [p[1], p[2], p[3]], F32R) for p in PIECES if p[4]}
        whole = {name: sb(f"w_{name}", [p, n, C]) for name, p, n in WHOLE}
        raw = [sb(f"raw{i}", [128, RING_COLS]) for i in range(RING)]
        ident = sb("ident", [128, 128], F32R)
        ones_e = sb("ones_e", [TP, EXPERTS])
        columns = sb("columns", [128, sum(n for _, n in COLUMNS)])
        column, k = {}, 0
        for name, n in COLUMNS:
            column[name] = columns[:, k:k + n]
            k += n
        ident32 = column["ident"]
        ln_w, ln_b = (column[n].rearrange("p (n k) -> p n k", k=2) for n in ("ln_w", "ln_b"))
        egb, eub, sgb, sub_ = (column[n] for n in ("egb", "eub", "sgb", "sub"))
        decay, first = column["decay"], column["first"]
        router_rows = sb("router_rows", [TP, 2 * EXPERTS + EGROUPS * EGROUPS])
        rbias, cbias = router_rows[:, 0:EXPERTS], router_rows[:, EXPERTS:2 * EXPERTS]
        before = router_rows[:, 2 * EXPERTS:].rearrange("p (i j) -> p i j", j=EGROUPS)
        dec_f, dec_b = sb("dec_f", [128, WK]), sb("dec_b", [128, WK])
        nothing, spare_v = sb("nothing", [128, len(PIECES)]), sb("spare_v", [128, 8])
        pat = sb("pat", [128, 2, N])
        h0, x0 = (sb(n, [TP, TILES, C]) for n in ("h0", "x0"))
        x1, base, gate_r, h1 = (sb(n, [TP, TILES, C]) for n in ("x1", "base", "gate_r", "h1"))
        rows_out = sb("rows_out", [TP, TILES, C])
        norm = [None, *(sb(f"norm{i}", [TP, TILES, 256]) for i in (1, 2))]
        full = [None, *(sb(f"full{i}", [128, 2, N]) for i in (1, 2))]
        norm.append(norm[2])
        full.append(full[2])
        stack = [None, *(sb(f"stack{i}", [128, 3, N], F32R) for i in (1, 2, 3))]
        stack_e = sb("stack_e", [128, 3, N], F32R)
        small = [None, *(dict((n, sb(n + i, shape, dt)) for n, shape, dt in (
            ("stats", [TP, TILES, 6], F32), ("mv", [TP, TILES, 2], F32), ("var", [TP, 2, TILES], F32),
            ("rstd", [TP, 2, TILES], F32), ("ny", [TP, 2, TILES], F32), ("seed", [TP, 2, TILES], I32),
            ("shift", [TP, 2, TILES], F32))) for i in "123")]
        K, KF, V, R = (sb(n, [128, WK]) for n in ("K", "KF", "V", "R"))
        M = [sb("Mf", [128, WK + 1]), sb("Mb", [128, WK + 1])]
        E1 = [sb("E1f", [128, WK]), sb("E1b", [128, WK])]
        SB = [sb("SBf", [128, WK + 1]), sb("SBb", [128, WK + 1])]
        SA = [sb("SAf", [128, WK + 1]), sb("SAb", [128, WK + 1])]
        top, own = sb("top", [128, WK]), sb("own", [128, WK])
        Z = sb("Z", [128, 2, N])
        AFTER = (slice(1, WK + 1), slice(0, WK))
        BEFORE = (slice(0, WK), slice(1, WK + 1))
        act, hid = sb("act", [128, 2, N]), sb("hid", [128, 2, N])
        relu, mix_hid = sb("relu", [128, N]), sb("mix_hid", [128, 2, N])
        sc, sfc, tmp_e, sel_e, eqs = (sb(n, [TP, TILES, EXPERTS]) for n in ("sc", "sfc", "tmp_e", "sel_e", "eqs"))
        pa, pb2, pc, pd = (sb(n, [TP, TILES, EGROUPS]) for n in ("pa", "pb2", "pc", "pd"))
        cmp1, cmp2 = (sb(n, [TP, TILES, EGROUPS, EGROUPS]) for n in ("cmp1", "cmp2"))
        top8 = sb("top8", [TP, TILES, 8])
        cnt = sb("cnt", [TP, TILES])
        ones48 = sb("ones48", [TP, TILES, CROWS])
        c48 = sb("c48", [TP, TILES, CROWS], F32R)
        cT = sb("cT", [CROWS, N], F32R)

        PF = pb("PF", [128, 2, 512])
        PQ = pb("PQ", [128, 512])
        PG = pb("PG", [128, 3, 512])
        PA = pb("PA", [128, 2, 512])

        raw_in = [sem(f"raw_in{i}") for i in range(RING)]
        hi_done, lo_done = sem("hi_done"), sem("lo_done")
        consts_in = sem("consts_in")
        consts_done = sem("consts_done")
        setup_v = sem("setup_v")
        whole_in = {name: sem(f"in_{name}") for name, _, _ in WHOLE}
        rstd_ready, act_norm, norm_ready, pe_transposed, act_high, act_full, stack_ready = (
            [None, *(counted(f"{n}{i}", k) for i in (1, 2, 3))] for n, k in (
                ("rstd_ready", 1), ("act_norm", TILES), ("norm_ready", 1), ("pe_transposed", 2),
                ("act_high", 2), ("act_full", 2), ("stack_ready", 2)))
        pat_in = counted("pat_in", 16)
        pe_tok = counted("pe_tok", 1)
        tok_out = counted("tok_out", 2)
        act_x0 = counted("act_x0", TILES)
        pe_kvr = counted("pe_kvr", 3)
        act_kvr = counted("act_kvr", 3)
        act_kf = counted("act_kf", 2)
        exp_in = counted("exp_in", 5)
        exp_out = counted("exp_out", 9)
        act_er = counted("act_er", 1)
        z_ready = counted("z_ready", 3)
        pe_o = counted("pe_o", 1)
        x1_ready = counted("x1_ready", 1)
        front_step = counted("front_step", FRONT_STEPS)
        pe_rf = counted("pe_rf", 1)
        act_rf = counted("act_rf", 1)
        pe_up = counted("pe_up", UPS)
        act_relu = counted("act_relu", UPS)
        act_square = counted("act_square", UPS)
        pe_mix = counted("pe_mix", UPS)
        pe_router = counted("pe_router", 1)
        logits_ready = counted("logits_ready", 1)
        act_score = counted("act_score", 1)
        c_ready = counted("c_ready", 1)
        mid_step = counted("mid_step", MID_STEPS)
        pe_cT = counted("pe_cT", 1)
        act_cT = counted("act_cT", 1)
        act_moved = counted("act_moved", 2)
        pe_gate = counted("pe_gate", SCH + ECH)
        pe_value = counted("pe_value", SCH + ECH)
        act_silu = counted("act_silu", SCH + ECH)
        gates_done = counted("gates_done", 2 * ECH)
        hid_ready = counted("hid_ready", SCH + ECH)
        pe_down = counted("pe_down", SCH + ECH, 1)
        out_ready = counted("out_ready", 2, 1)
        out_stored = counted("out_stored", 16 * TILES, 1)
        block = ctx.enter_context(nc.Block())

        BANKS = ((0, 0, 2), (1, 2, 3))

        def rows(P, bank, a, b):
            return P[0:TP, bank, 0:(b - a) * C].rearrange("p (t c) -> p t c", c=C)

        def tile_out(P, t):
            return P[0:TP, t // 2, (t % 2) * C:(t % 2 + 1) * C]

        def since(engine, s, g):
            if not (isinstance(g, int) and g == 0):
                engine.wait_ge(s, at(s, g, 0))

        @block.sync
        def _(sp):
            def piece(n):
                name, prt, slots, cols, _ = PIECES[n]
                if n >= RING:
                    sp.wait_ge(lo_done, n - RING + 1)
                sp.dma_start(raw[n % RING][0:prt, 0:slots * cols],
                             A[f"w_{name}"]).then_inc(raw_in[n % RING], 16)

            def unsplit(name):
                sp.dma_start(whole[name][:, :, :], A[f"w_{name}"]).then_inc(whole_in[name], 16)

            def patches(g):
                sp.dma_start(pat[:, :, :], A["patches"][bass.ds(g, 1)].rearrange("a p k n -> (a p) k n")).then_inc(pat_in, 16)

            def store(g):
                sp.wait_ge(out_ready, at(out_ready, g, 2))
                for t in range(TILES):
                    skip = TS[t - 1] + TP - TS[t] if t else 0
                    sp.dma_start(A["out"][bass.ds(g, 1), TS[t] + skip:TS[t] + TP, :].rearrange("a p c -> (a p) c"),
                                 rows_out[skip:TP, t, :]).then_inc(out_stored, 16)

            patches(0)
            unsplit("tok")
            for n in range(4):
                piece(n)
            unsplit("o")
            for n in range(4, 8):
                piece(n)
            unsplit("down")
            sp.wait_ge(pe_tok, at(pe_tok, 0, 1))
            patches(1)
            for n in range(8, 10):
                piece(n)
            unsplit("sd")
            for n in range(10, 13):
                piece(n)
            unsplit("ed")
            for n in range(13, len(PIECES)):
                piece(n)
            with sp.Fori(2, GROUPS) as g:
                sp.wait_ge(pe_tok, at(pe_tok, g - 1, 1))
                patches(g)
            with sp.Fori(0, GROUPS) as g:
                store(g)
            sp.wait_ge(out_stored, at(out_stored, GROUPS, 0))

        @block.gpsimd
        def _(pool):
            for n, (name, prt, slots, cols, has_lo) in enumerate(PIECES):
                src = raw[n % RING][0:prt, 0:slots * cols].rearrange("p (s c) -> p s c", s=slots)
                pool.wait_ge(hi_done, n + 1)
                if n:
                    pool.wait_ge(lo_done, n)
                if name in ("bd", "cls"):
                    low = slice(32, 64) if name == "bd" else slice(32, CLS)
                    nc.gpsimd.tensor_tensor(hi[name][low, :, :], src[low], hi[name][low, :, :].bitcast(F32),
                                            ALU.subtract).then_inc(lo_done, 1)
                elif not has_lo:
                    nc.gpsimd.memset(nothing[:, n:n + 1], 0.0).then_inc(lo_done, 1)
                else:
                    nc.gpsimd.tensor_tensor(lo[name][:, :, :], src, hi[name][:, :, :].bitcast(F32),
                                            ALU.subtract).then_inc(lo_done, 1)

        def advance(tracks, order):
            for track, upto in order:
                if track not in tracks:
                    continue
                if isinstance(upto, int):
                    for _ in range(upto):
                        next(tracks[track], None)
                else:
                    for name in tracks[track]:
                        if name == upto:
                            break
            for rest in tracks.values():
                for _ in rest:
                    pass

        def pipeline(engine, tracks, order):
            advance({name: tracks[name](engine, 0) for name in ("F", "W") if name in tracks}, order)
            advance({"F": tracks["F"](engine, 1), "M": tracks["M"](engine, 0)}, order)
            with engine.Fori(0, GROUPS - 2) as g:
                advance({"Y": tracks["Y"](engine, g), "M": tracks["M"](engine, g + 1), "F": tracks["F"](engine, g + 2)}, order)
            advance({"Y": tracks["Y"](engine, GROUPS - 2), "M": tracks["M"](engine, GROUPS - 1, False)}, order)
            advance({"Y": tracks["Y"](engine, GROUPS - 1)}, order)


        def act_high_parts(act_e):
            for n, (name, prt, slots, cols, _) in enumerate(PIECES):
                act_e.wait_ge(raw_in[n % RING], 16 * (n // RING + 1))
                nc.scalar.activation(hi[name][:, :, :], raw[n % RING][0:prt, 0:slots * cols].rearrange("p (s c) -> p s c", s=slots),
                                     ACT.Copy).then_inc(hi_done, 1)
                yield

        def act_norm_rows(act_e, g, n, x, col=0):
            for t in range(TILES):
                nc.scalar.activation(norm[n][:, t, 0:C], x[:, t, :], ACT.Identity, bias=small[n]["shift"][:, col, t:t + 1],
                                     scale=small[n]["rstd"][:, col, t:t + 1]).then_inc(act_norm[n], 1)
            act_e.wait_ge(act_norm[n], at(act_norm[n], g, TILES))
            nc.scalar.activation(norm[n][:, :, C:256], norm[n][:, :, 128:C], ACT.Copy).then_inc(norm_ready[n], 1)

        def act_stack(act_e, g, n, affine):
            for k in range(2):
                act_e.wait_ge(pe_transposed[n], at(pe_transposed[n], g, k + 1))
                for dst, done in ((stack[n], act_high[n]), (full[n], act_full[n])):
                    if affine:
                        nc.scalar.activation(dst[:, k, :], PF[:, k, 0:N], ACT.Identity, bias=ln_b[:, n - 1, k:k + 1],
                                             scale=ln_w[:, n - 1, k:k + 1]).then_inc(done, 1)
                    else:
                        nc.scalar.activation(dst[:, k, :], PF[:, k, 0:N], ACT.Copy).then_inc(done, 1)

        def act_front(act_e, g):
            act_e.wait_ge(pe_tok, at(pe_tok, g, 1))
            since(act_e, x1_ready, g)
            for bank, a, b in BANKS:
                nc.scalar.activation(h0[:, a:b, :], rows(PF, bank, a, b), ACT.Copy).then_inc(tok_out, 1)
            yield "tok"
            if isinstance(g, int) and g == 0:
                act_e.wait_ge(consts_done, 1)
            act_e.wait_ge(rstd_ready[1], at(rstd_ready[1], g, 1))
            act_norm_rows(act_e, g, 1, h0, 1)
            yield "ln1"
            act_stack(act_e, g, 1, True)
            yield "tr1"
            for n, dst in enumerate((K, V, R)):
                act_e.wait_ge(pe_kvr, at(pe_kvr, g, n + 1))
                if n == 0:
                    for h, s in enumerate(BLOCKS):
                        nc.scalar.activation(KF[:, s], PF[:, 0, s], ACT.Identity, bias=first[:, h:h + 1]).then_inc(act_kf, 1)
                nc.scalar.activation(dst[:, :], PF[:, n % 2, 0:WK], ACT.Copy).then_inc(act_kvr, 1)
                yield "kvr"[n]
            act_e.wait_ge(act_kvr, at(act_kvr, g, 3))
            act_e.wait_ge(exp_in, at(exp_in, g, 1))
            for d in range(2):
                act_e.wait_ge(exp_in, at(exp_in, g, d + 1))
                for h, s in enumerate(BLOCKS):
                    nc.scalar.activation(E1[d][:, s], E1[d][:, s], ACT.Exp, bias=decay[:, h:h + 1]).then_inc(exp_out, 1)
                nc.scalar.activation(SB[d][:, AFTER[d]], SB[d][:, AFTER[d]], ACT.Exp).then_inc(exp_out, 1)
            for n, a in enumerate((M[0][:, BEFORE[0]], M[1][:, BEFORE[1]], own[:, :])):
                act_e.wait_ge(exp_in, at(exp_in, g, n + 3))
                nc.scalar.activation(a, a, ACT.Exp).then_inc(exp_out, 1)
            nc.scalar.activation(R[:, :], R[:, :], ACT.Exp, scale=-1.0).then_inc(act_er, 1)
            yield "exps"
            for t in range(TILES):
                nc.scalar.activation(x0[:, t, :], h0[:, t, :], ACT.Identity, bias=small[1]["shift"][:, 0, t:t + 1],
                                     scale=small[1]["rstd"][:, 0, t:t + 1]).then_inc(act_x0, 1)
            yield "x0"

        def act_mid(act_e, g, beside=True):
            act_e.wait_ge(rstd_ready[2], at(rstd_ready[2], g, 1))
            act_norm_rows(act_e, g, 2, x1)
            yield "ln2"
            act_stack(act_e, g, 2, True)
            yield "tr2"
            act_e.wait_ge(pe_rf, at(pe_rf, g, 1))
            for bank, a, b in BANKS:
                last = nc.scalar.activation(gate_r[:, a:b, :], rows(PF, bank, a, b), ACT.Tanh, scale=0.5)
            last.then_inc(act_rf, 1)
            yield "rf"
            for m in range(UPS):
                act_e.wait_ge(pe_up, at(pe_up, g, m + 1))
                if m == 0:
                    since(act_e, act_square, g)
                else:
                    act_e.wait_ge(act_square, at(act_square, g, m))
                nc.scalar.activation(relu[:, :], PQ[:, 0:N], ACT.Relu).then_inc(act_relu, 1)
                act_e.wait_ge(act_relu, at(act_relu, g, m + 1))
                if m >= 2:
                    act_e.wait_ge(pe_mix, at(pe_mix, g, m - 1))
                elif m == 0:
                    since(act_e, pe_mix, g)
                nc.scalar.activation(mix_hid[:, m % 2, :], relu[:, :], ACT.Square).then_inc(act_square, 1)
                yield f"mix{m}"
            yield "mixed"
            act_e.wait_ge(rstd_ready[3], at(rstd_ready[3], g, 1))
            act_norm_rows(act_e, g, 3, h1)
            yield "ln3"
            since(act_e, act_moved, g)
            act_stack(act_e, g, 3, False)
            yield "tr3"
            act_e.wait_ge(logits_ready, at(logits_ready, g, 1))
            nc.scalar.activation(sc[:, :, :], sc[:, :, :], ACT.Tanh, scale=0.5).then_inc(act_score, 1)
            yield "logits"

        def act_experts(act_e, g):
            act_e.wait_ge(pe_down, at(pe_down, g, 0))
            act_e.wait_ge(stack_ready[3], at(stack_ready[3], g, 2))
            nc.scalar.activation(stack_e[:, :, :], stack[3][:, :, :].bitcast(F32), ACT.Copy).then_inc(act_moved, 1)
            yield "stack"
            act_e.wait_ge(pe_cT, at(pe_cT, g, 1))
            nc.scalar.activation(cT[:, :], PQ[0:CROWS, 0:N], ACT.Copy).then_inc(act_cT, 1)
            act_e.wait_ge(out_stored, at(out_stored, g, 0))
            nc.scalar.activation(rows_out[:, :, :], h1[:, :, :], ACT.Copy).then_inc(act_moved, 1)
            yield "load"
            yield "first"
            for n in range(SCH + ECH):
                prt, bias = (INNER, sgb[0:INNER, n:n + 1]) if n < SCH else (128, egb[:, n - SCH:n - SCH + 1])
                act_e.wait_ge(pe_gate, at(pe_gate, g, n + 1))
                if n >= 2:
                    act_e.wait_ge(hid_ready, at(hid_ready, g, n - 1))
                nc.scalar.activation(act[0:prt, n % 2, :], PG[0:prt, 2 * n % 3, 0:N], ACT.Silu, bias=bias).then_inc(act_silu, 1)
                yield f"e{n}"

        @block.scalar
        def _(act_e):
            act_e.dma_start(columns[:, :], A["columns"]).then_inc(consts_in, 16)
            act_e.dma_start(router_rows[:, :], A["router_rows"].broadcast_to([TP, 2 * EXPERTS + EGROUPS * EGROUPS])).then_inc(consts_in, 16)
            high = act_high_parts(act_e)

            def weights(act_e, g):
                yield from high

            pipeline(act_e, {"F": act_front, "M": act_mid, "Y": act_experts, "W": weights}, ACT_ORDER)

        V_ = nc.vector

        def stepper(v, g, sem, spare):
            count, spares = [0], [0]

            def step(ins):
                count[0] += 1
                ins.then_inc(sem, 1)

            def settle():
                v.wait_ge(sem, at(sem, g, count[0]))

            def do(ins):
                step(ins)
                settle()

            def settle_apart():
                settle()
                V_.memset(spare[:, spares[0]:spares[0] + 1], 0.0)
                spares[0] += 1

            return step, settle, do, settle_apart, count

        def moments(steps, n, x):
            step, settle, do, settle_apart, _ = steps
            stats, mv, var = (small[n][k] for k in ("stats", "mv", "var"))
            for t in range(TILES):
                step(V_.bn_stats(stats[:, t, :], x[:, t, :]))
            settle_apart()
            for t in range(TILES):
                step(V_.bn_aggr(mv[:, t, :], stats[:, t, :]))
            yield
            settle()
            step(V_.tensor_scalar(var[:, 0, :], mv[:, :, 1], EPS, None, ALU.add))
            yield
            settle()

        def rsqrt(steps, n, cols):
            step, settle, do, _, _ = steps
            var, rstd, ny, seed = (small[n][k][:, 0:cols, :] for k in ("var", "rstd", "ny", "seed"))
            step(V_.tensor_scalar(seed, var.bitcast(I32), 1, None, ALU.logical_shift_right))
            yield
            settle()
            step(V_.tensor_scalar(rstd.bitcast(I32), seed, -1.0, RSQRT_SEED, ALU.mult, ALU.add))
            yield
            settle()
            for _ in range(3):
                step(V_.tensor_tensor(ny, rstd, rstd, ALU.mult))
                yield
                settle()
                step(V_.scalar_tensor_tensor(ny, ny, -0.5, var, ALU.mult, ALU.mult))
                yield
                settle()
                step(V_.scalar_tensor_tensor(rstd, ny, 1.5, rstd, ALU.add, ALU.mult))
                yield
                settle()

        def shift_rows(n):
            V_.scalar_tensor_tensor(small[n]["shift"][:, 0, :], small[n]["mv"][:, :, 0], -1.0, small[n]["rstd"][:, 0, :],
                                    ALU.mult, ALU.mult).then_inc(rstd_ready[n], 1)

        def split_low(v, g, n):
            v.wait_ge(act_high[n], at(act_high[n], g, 2))
            v.wait_ge(act_full[n], at(act_full[n], g, 2))
            V_.tensor_tensor(stack[n][:, 2, :], full[n][:, 0, :], stack[n][:, 0, :].bitcast(F32), ALU.subtract).then_inc(stack_ready[n], 1)
            up = slice(64, 128)
            V_.tensor_tensor(stack[n][up, 1, :], full[n][up, 1, :], stack[n][up, 1, :].bitcast(F32), ALU.subtract).then_inc(stack_ready[n], 1)

        def dve_front(v, g):
            steps = stepper(v, g, front_step, spare_v[:, 0:4])
            step, settle, do, settle_apart, count = steps
            mv, var, rstd, shift = (small[1][k] for k in ("mv", "var", "rstd", "shift"))
            v.wait_ge(tok_out, at(tok_out, g, 2))
            yield from moments(steps, 1, h0)
            step(V_.reciprocal(var[:, 1, :], var[:, 0, :]))
            yield
            settle()
            step(V_.tensor_tensor(var[:, 1, :], var[:, 1, :], mv[:, :, 1], ALU.mult))
            yield
            settle()
            do(V_.tensor_scalar(var[:, 1, :], var[:, 1, :], EPS, None, ALU.add))
            yield from rsqrt(steps, 1, 2)
            step(V_.tensor_tensor(rstd[:, 1, :], rstd[:, 0, :], rstd[:, 1, :], ALU.mult))
            yield
            settle()
            V_.scalar_tensor_tensor(shift[:, :, :], mv[:, None, :, 0].broadcast_to([TP, 2, TILES]), -1.0, rstd[:, :, :],
                                    ALU.mult, ALU.mult).then_inc(rstd_ready[1], 1)
            yield "ln1"
            split_low(v, g, 1)
            yield "tr1"

            def run(x, d):
                return x if d == 0 else x[:, ::-1]

            v.wait_ge(act_kvr, at(act_kvr, g, 1))
            for d, dec in enumerate((dec_f, dec_b)):
                step(V_.tensor_tensor_scan(run(M[d][:, AFTER[d]], d), run(dec[:, :], d), run(K[:, :], d), 0.0, ALU.add, ALU.max))
                yield
            for d in range(2):
                settle()
                old, new = M[d][:, BEFORE[d]], M[d][:, AFTER[d]]
                step(V_.tensor_tensor(E1[d][:, :], old, new, ALU.subtract))
                yield
                step(V_.tensor_tensor(SB[d][:, AFTER[d]], K[:, :], new, ALU.subtract))
                yield
                settle()
                start = 0 if d == 0 else T - 1
                do(V_.memset(old[:, start::T], NEG))
                V_.memset(E1[d][:, start::T], NEG).then_inc(exp_in, 1)
                yield "maxima"
            mf, mb = M[0][:, BEFORE[0]], M[1][:, BEFORE[1]]
            step(V_.tensor_tensor(top[:, :], mf, mb, ALU.max))
            yield
            settle()
            v.wait_ge(act_kf, at(act_kf, g, 2))
            step(V_.tensor_tensor(top[:, :], KF[:, :], top[:, :], ALU.max))
            yield
            settle()
            V_.tensor_tensor(mf, mf, top[:, :], ALU.subtract).then_inc(exp_in, 1)
            yield
            V_.tensor_tensor(mb, mb, top[:, :], ALU.subtract).then_inc(exp_in, 1)
            yield
            V_.tensor_tensor(own[:, :], KF[:, :], top[:, :], ALU.subtract).then_inc(exp_in, 1)
            yield "exps"
            v.wait_ge(act_kvr, at(act_kvr, g, 2))
            for d in range(2):
                v.wait_ge(exp_out, at(exp_out, g, 3 * d + 3))
                a, b = SA[d][:, AFTER[d]], SB[d][:, AFTER[d]]
                step(V_.tensor_tensor(a, b, V[:, :], ALU.mult))
                yield
                settle()
                step(V_.tensor_tensor_scan(run(a, d), run(E1[d][:, :], d), run(a, d), 0.0, ALU.mult, ALU.add))
                yield
                step(V_.tensor_tensor_scan(run(b, d), run(E1[d][:, :], d), run(b, d), 0.0, ALU.mult, ALU.add))
                yield
                settle()
            for d in range(2):
                v.wait_ge(exp_out, at(exp_out, g, 7 + d))
                for x in (SA[d], SB[d]):
                    step(V_.tensor_tensor(x[:, BEFORE[d]], x[:, BEFORE[d]], M[d][:, BEFORE[d]], ALU.mult))
                    yield
            v.wait_ge(exp_out, at(exp_out, g, 9))
            step(V_.tensor_tensor(V[:, :], V[:, :], own[:, :], ALU.mult))
            yield
            settle()
            step(V_.tensor_tensor(top[:, :], SA[0][:, BEFORE[0]], SA[1][:, BEFORE[1]], ALU.add))
            yield
            step(V_.tensor_tensor(K[:, :], SB[0][:, BEFORE[0]], SB[1][:, BEFORE[1]], ALU.add))
            yield
            settle()
            step(V_.tensor_tensor(top[:, :], top[:, :], V[:, :], ALU.add))
            yield
            step(V_.tensor_tensor(K[:, :], K[:, :], own[:, :], ALU.add))
            yield
            settle()
            v.wait_ge(act_er, at(act_er, g, 1))
            step(V_.scalar_tensor_tensor(K[:, :], R[:, :], 1.0, K[:, :], ALU.add, ALU.mult))
            yield
            settle()
            for s in BLOCKS:
                step(V_.reciprocal(K[:, s], K[:, s]))
                yield
            settle()
            for z, x in ((Z[:, 0, :], (slice(0, 128), BLOCKS[0])),
                         (Z[0:64, 1, 0:NB], (slice(0, 64), BLOCKS[1])), (Z[64:128, 1, NB:N], (slice(64, 128), BLOCKS[1]))):
                V_.tensor_tensor(z, K[x], top[x], ALU.mult).then_inc(z_ready, 1)
            yield "z"

            v.wait_ge(pe_o, at(pe_o, g, 1))
            v.wait_ge(act_x0, at(act_x0, g, TILES))
            since(v, norm_ready[3], g)
            for bank, a, b in BANKS:
                step(V_.tensor_tensor(x1[:, a:b, :], x0[:, a:b, :], rows(PF, bank, a, b), ALU.add))
            yield
            settle()
            V_.tensor_tensor(base[:, :, :], h0[:, :, :], x1[:, :, :], ALU.add).then_inc(x1_ready, 1)
            assert count[0] == per_group[front_step], count
            yield "x1"

        def dve_mid(v, g, beside=True):
            steps = stepper(v, g, mid_step, spare_v[:, 4:8])
            step, settle, do, settle_apart, count = steps
            v.wait_ge(x1_ready, at(x1_ready, g, 1))
            yield from moments(steps, 2, x1)
            yield from rsqrt(steps, 2, 1)
            shift_rows(2)
            yield "ln2"
            split_low(v, g, 2)
            yield "tr2"
            v.wait_ge(act_rf, at(act_rf, g, 1))
            v.wait_ge(pe_mix, at(pe_mix, g, UPS))
            since(v, act_moved, g)
            for bank, a, b in BANKS:
                step(V_.scalar_tensor_tensor(gate_r[:, a:b, :], gate_r[:, a:b, :], 1.0, rows(PF, bank, a, b), ALU.add, ALU.mult))
            yield
            settle()
            step(V_.scalar_tensor_tensor(h1[:, :, :], gate_r[:, :, :], 0.5, base[:, :, :], ALU.mult, ALU.add))
            yield
            settle()
            yield from moments(steps, 3, h1)
            yield from rsqrt(steps, 3, 1)
            shift_rows(3)
            yield "ln3"
            split_low(v, g, 3)
            yield "tr3"
            v.wait_ge(pe_router, at(pe_router, g, 1))
            E3 = [TP, TILES, EXPERTS]
            V_.tensor_tensor(sc[:, :, :], PQ[0:TP, 0:TILES * EXPERTS].rearrange("p (t e) -> p t e", e=EXPERTS),
                             rbias[:, None, :].broadcast_to(E3), ALU.add).then_inc(logits_ready, 1)
            yield "logits"
            v.wait_ge(act_score, at(act_score, g, 1))
            do(V_.tensor_scalar(sc[:, :, :], sc[:, :, :], 1.0, 0.5, ALU.add, ALU.mult))
            step(V_.tensor_tensor(sfc[:, :, :], sc[:, :, :], cbias[:, None, :].broadcast_to(E3), ALU.add))
            yield
            settle()
            quad = sfc[:, :, :].rearrange("p t (g e) -> p t g e", e=EPG)
            q = [quad[:, :, :, i] for i in range(EPG)]
            P_, S_ = tmp_e[:, :, 0:EGROUPS], tmp_e[:, :, EGROUPS:2 * EGROUPS]
            step(V_.tensor_tensor(pa[:, :, :], q[0], q[1], ALU.max))
            step(V_.tensor_tensor(pb2[:, :, :], q[0], q[1], ALU.min))
            step(V_.tensor_tensor(pc[:, :, :], q[2], q[3], ALU.max))
            step(V_.tensor_tensor(pd[:, :, :], q[2], q[3], ALU.min))
            settle()
            step(V_.tensor_tensor(P_, pa[:, :, :], pc[:, :, :], ALU.max))
            step(V_.tensor_tensor(S_, pa[:, :, :], pc[:, :, :], ALU.min))
            do(V_.tensor_tensor(pb2[:, :, :], pb2[:, :, :], pd[:, :, :], ALU.max))
            step(V_.tensor_tensor(S_, S_, pb2[:, :, :], ALU.max))
            yield
            settle()
            step(V_.tensor_tensor(pa[:, :, :], P_, S_, ALU.add))
            yield
            settle()
            G4 = [TP, TILES, EGROUPS, EGROUPS]
            other, mine = pa[:, :, None, :].broadcast_to(G4), pa[:, :, :, None].broadcast_to(G4)
            step(V_.tensor_tensor(cmp1[:, :, :, :], other, mine, ALU.is_gt))
            step(V_.tensor_tensor(cmp2[:, :, :, :], other, mine, ALU.is_equal))
            yield
            settle()
            step(V_.tensor_tensor(cmp2[:, :, :, :], cmp2[:, :, :, :], before[:, None, :, :].broadcast_to(G4), ALU.mult))
            yield
            settle()
            step(V_.tensor_tensor(cmp1[:, :, :, :], cmp1[:, :, :, :], cmp2[:, :, :, :], ALU.add))
            yield
            settle()
            step(V_.tensor_reduce(pa[:, :, :], cmp1[:, :, :, :], AXX, ALU.add))
            yield
            settle()
            step(V_.tensor_scalar(pa[:, :, :], pa[:, :, :], float(TOPG), None, ALU.is_lt))
            yield
            settle()
            step(V_.tensor_tensor(quad, quad, pa[:, :, :, None].broadcast_to([TP, TILES, EGROUPS, EPG]), ALU.mult))
            settle_apart()
            for t in range(TILES):
                step(V_.max(top8[:, t, :], sfc[:, t, :]))
            yield
            settle()
            fourth = top8[:, :, TOPK - 1:TOPK].broadcast_to(E3)
            step(V_.tensor_tensor(sel_e[:, :, :], sfc[:, :, :], fourth, ALU.is_gt))
            step(V_.tensor_tensor(eqs[:, :, :], sfc[:, :, :], fourth, ALU.is_equal))
            yield
            settle()
            step(V_.tensor_reduce(cnt[:, :], sel_e[:, :, :], AXX, ALU.add))
            yield
            settle()
            for t in range(TILES):
                step(V_.tensor_tensor_scan(tmp_e[:, t, :], ones_e[:, :], eqs[:, t, :], cnt[:, t:t + 1], ALU.mult, ALU.add))
            yield
            settle()
            step(V_.scalar_tensor_tensor(tmp_e[:, :, :], tmp_e[:, :, :], float(TOPK), eqs[:, :, :], ALU.is_le, ALU.mult))
            yield
            settle()
            step(V_.tensor_tensor(sel_e[:, :, :], sel_e[:, :, :], tmp_e[:, :, :], ALU.add))
            yield
            settle()
            step(V_.tensor_tensor(sc[:, :, :], sc[:, :, :], sel_e[:, :, :], ALU.mult))
            yield
            settle()
            step(V_.tensor_reduce(cnt[:, :], sc[:, :, :], AXX, ALU.add))
            yield
            settle()
            do(V_.tensor_scalar(cnt[:, :], cnt[:, :], 1e-20, None, ALU.add))
            step(V_.reciprocal(cnt[:, :], cnt[:, :]))
            yield
            settle()
            step(V_.scalar_tensor_tensor(sc[:, :, :], sc[:, :, :], SCALE, cnt[:, :, None].broadcast_to(E3), ALU.mult, ALU.mult))
            yield
            settle()
            since(v, pe_cT, g)
            step(V_.tensor_copy(c48[:, :, 0:EXPERTS], sc[:, :, :]))
            do(V_.tensor_copy(c48[:, :, 2 * EXPERTS:3 * EXPERTS], sc[:, :, :]))
            V_.tensor_tensor(c48[:, :, EXPERTS:2 * EXPERTS], sc[:, :, :], c48[:, :, 0:EXPERTS].bitcast(F32),
                             ALU.subtract).then_inc(c_ready, 1)
            assert count[0] == per_group[mid_step], count
            yield "routed"

        def dve_experts(v, g):
            yield "load"
            for n in range(SCH + ECH):
                i, prt, bank = n % 2, INNER if n < SCH else 128, (2 * n + 1) % 3
                v.wait_ge(act_silu, at(act_silu, g, n + 1))
                v.wait_ge(pe_value, at(pe_value, g, n + 1))
                if n < SCH:
                    bias = sub_[0:INNER, n:n + 1]
                else:
                    bias = eub[:, n - SCH:n - SCH + 1]
                    first_bank, j = 2 * n % 3, n - SCH
                    if first_bank < 2:
                        gates = act[:, i, :].rearrange("p (h n) -> p h n", h=2)
                        V_.tensor_tensor(gates, gates, PG[:, first_bank:first_bank + 2, N:N + NB], ALU.mult).then_inc(gates_done, 2)
                    else:
                        for h, b in enumerate((2, 0)):
                            gates = act[:, i, h * NB:(h + 1) * NB]
                            V_.tensor_tensor(gates, gates, PG[:, b, N:N + NB], ALU.mult).then_inc(gates_done, 1)
                    v.wait_ge(gates_done, at(gates_done, g, 2 * j + 2))
                if n >= 2:
                    v.wait_ge(pe_down, at(pe_down, g, n - 1))
                V_.scalar_tensor_tensor(hid[0:prt, i, :], PG[0:prt, bank, 0:N], bias, act[0:prt, i, :],
                                        ALU.add, ALU.mult).then_inc(hid_ready, 1)
                yield f"e{n}"
            v.wait_ge(pe_down, at(pe_down, g, SCH + ECH))
            v.wait_ge(act_moved, at(act_moved, g, 2))
            for bank, a, b in BANKS:
                V_.tensor_tensor(rows_out[:, a:b, :], rows_out[:, a:b, :], rows(PA, bank, a, b), ALU.add).then_inc(out_ready, 1)
            yield "end"

        @block.vector
        def _(v):
            count = [0]

            def setup(ins):
                count[0] += 1
                ins.then_inc(setup_v, 1)

            for d in range(2):
                edge = 0 if d == 0 else WK
                for a in (M[d], SA[d], SB[d]):
                    setup(nc.vector.memset(a[:, edge:edge + 1], 0.0))
            nc.vector.memset(spare_v[:, 2:3], 0.0).then_inc(out_ready, 1)
            nc.vector.memset(spare_v[:, 3:4], 0.0).then_inc(out_stored, 1)
            nc.vector.memset(spare_v[:, 1:2], 0.0).then_inc(pe_down, 1)
            setup(nc.vector.memset(own[:, :], 0.0))
            setup(nc.vector.memset(ones_e[:, :], 1.0))
            setup(nc.vector.memset(Z[:, 1, :], 0.0))
            setup(nc.vector.memset(ones48[:, :, :], 0.0))
            v.wait_ge(setup_v, count[0])
            for row in (3 * EXPERTS, 64):
                setup(nc.vector.memset(ones48[:, :, row:row + 1], 1.0))
            v.wait_ge(setup_v, count[0])
            setup(nc.vector.tensor_copy(c48[:, :, :], ones48[:, :, :]))
            v.wait_ge(consts_in, 16 * 2)
            setup(nc.vector.tensor_copy(ident[:, :], ident32[:, :]))
            setup(nc.vector.tensor_scalar(decay[:, :], decay[:, :], 1.0 / T, None, ALU.mult))
            setup(nc.vector.tensor_scalar(first[:, :], first[:, :], 1.0 / T, None, ALU.mult))
            v.wait_ge(setup_v, count[0])
            for a in (dec_f, dec_b):
                for h, s in enumerate(BLOCKS):
                    setup(nc.vector.tensor_scalar(a[:, s], own[:, s], decay[:, h:h + 1], None, ALU.add))
            v.wait_ge(setup_v, count[0])
            setup(nc.vector.memset(dec_f[:, 0:WK:T], NEG))
            nc.vector.memset(dec_b[:, T - 1:WK:T], NEG).then_inc(consts_done, 1)
            v.wait_ge(setup_v, count[0])
            v.wait_ge(consts_done, 1)
            pipeline(v, {"F": dve_front, "M": dve_mid, "Y": dve_experts}, DVE_ORDER)

        mm = nc.tensor.matmul

        def need(pe, name):
            pe.wait_ge(lo_done, PIECE_AT[name] + 1)

        def from_stack(out, x, name, cols, tokens=slice(0, N), opens=True, more=False):
            w_hi, w_lo = hi[name], lo[name]
            for p, slot in enumerate((0, 1, 0)):
                mm(out, w_hi[:, slot, cols], x[:, p, tokens], start=(opens and p == 0), stop=False, skip_group_check=True)
            for p in range(2):
                last = mm(out, w_lo[:, p, cols], x[:, p, tokens], start=False, stop=(p == 1 and not more), skip_group_check=True)
            return last

        def rows_from_stack(out, opens, x, name, cols):
            w_hi, w_lo = hi[name], lo[name]
            for t in range(TILES):
                for p, slot in enumerate((0, 1, 0)):
                    mm(out(t), x[:, p, TS[t]:TS[t] + TP], w_hi[:, slot, cols],
                       start=(p == 0 and t in opens), stop=False, skip_group_check=True)
                for p in range(2):
                    last = mm(out(t), x[:, p, TS[t]:TS[t] + TP], w_lo[:, p, cols],
                              start=False, stop=(p == 1), skip_group_check=True)
            return last

        def down(P, src, w, start, stop):
            for t in range(TILES):
                last = mm(tile_out(P, t), src[:, TS[t]:TS[t] + TP], w, start=start and t != 1, stop=stop, skip_group_check=True)
            return last

        def transposes(pe, g, n):
            pe.wait_ge(norm_ready[n], at(norm_ready[n], g, 1))
            for k in range(2):
                for t in range(TILES):
                    last = nc.tensor.transpose(PF[:, k, TS[t]:TS[t] + TP], norm[n][:, t, k * 128:(k + 1) * 128], ident32[0:TP, 0:TP])
                last.then_inc(pe_transposed[n], 1)

        def pe_front(pe, g):
            since(pe, x1_ready, g)
            pe.wait_ge(whole_in["tok"], 16)
            pe.wait_ge(pat_in, at(pat_in, g, 16))
            down(PF, pat[:, 0, :], whole["tok"][:, 0, :], True, False)
            down(PF, pat[:, 1, :], whole["tok"][:, 1, :], False, False)
            need(pe, "mask")
            down(PF, hi["mask"][:, 0, :], hi["cls"][:, 0, :], False, True).then_inc(pe_tok, 1)
            yield "tok"
            yield "ln1"
            if isinstance(g, int) and g == 0:
                pe.wait_ge(consts_done, 1)
            pe.wait_ge(tok_out, at(tok_out, g, 2))
            since(pe, act_full[2], g)
            transposes(pe, g, 1)
            yield "tr1"
            for n, name in enumerate(("k", "v", "r")):
                need(pe, name)
                if n == 0:
                    pe.wait_ge(stack_ready[1], at(stack_ready[1], g, 2))
                elif n == 2:
                    pe.wait_ge(act_kvr, at(act_kvr, g, 1))
                P = PF[:, n % 2, :]
                from_stack(P[:, 0:N], stack[1], name, slice(0, 128), more=True)
                for h in range(2):
                    last = from_stack(P[:, N:WK], stack[1], name, slice(128 + 64 * h, 256 + 64 * h),
                                      tokens=slice(h * NB, (h + 1) * NB), opens=False, more=(h == 0))
                last.then_inc(pe_kvr, 1)
                yield name
            yield "exps"
            pe.wait_ge(whole_in["o"], 16)
            pe.wait_ge(act_kvr, at(act_kvr, g, 3))
            since(pe, act_full[3], g)
            pe.wait_ge(z_ready, at(z_ready, g, 3))
            for h in range(2):
                last = down(PF, Z[:, h, :], whole["o"][:, h, :], h == 0, h == 1)
            last.then_inc(pe_o, 1)
            yield "o"

        def pe_mid(pe, g, beside=True):
            yield "ln2"
            if beside:
                pe.wait_ge(tok_out, at(tok_out, g + 1, 2))
            transposes(pe, g, 2)
            yield "tr2"
            pe.wait_ge(stack_ready[2], at(stack_ready[2], g, 2))
            if beside:
                pe.wait_ge(act_kvr, at(act_kvr, g + 1, 3))
            need(pe, "rf")
            rows_from_stack(lambda t: tile_out(PF, t), (0, 2), stack[2], "rf", slice(0, C)).then_inc(pe_rf, 1)
            yield "rf"

            def up(m):
                need(pe, f"up{m // 3}")
                if m == 0:
                    since(pe, act_cT, g)
                else:
                    pe.wait_ge(act_relu, at(act_relu, g, m))
                from_stack(PQ[:, 0:N], stack[2], f"up{m // 3}", slice(m % 3 * 128, (m % 3 + 1) * 128)).then_inc(pe_up, 1)

            def mix(m):
                if m == 0:
                    pe.wait_ge(act_rf, at(act_rf, g, 1))
                pe.wait_ge(act_square, at(act_square, g, m + 1))
                down(PF, mix_hid[:, m % 2, :], whole["down"][:, m, :], m == 0, m == UPS - 1).then_inc(pe_mix, 1)

            pe.wait_ge(whole_in["down"], 16)
            for m in range(UPS):
                up(m)
                if m:
                    mix(m - 1)
                yield f"mix{m}"
            mix(UPS - 1)
            yield "mixed"
            yield "ln3"
            transposes(pe, g, 3)
            yield "tr3"
            pe.wait_ge(stack_ready[3], at(stack_ready[3], g, 2))
            pe.wait_ge(act_relu, at(act_relu, g, UPS))
            need(pe, "router")
            rows_from_stack(lambda t: PQ[0:TP, t * EXPERTS:(t + 1) * EXPERTS], (0,), stack[3],
                            "router", slice(0, EXPERTS)).then_inc(pe_router, 1)
            yield "logits"

        def pe_experts(pe, g):
            pe.wait_ge(c_ready, at(c_ready, g, 1))
            for t in range(TILES):
                skip = TS[t - 1] + TP - TS[t] if t else 0
                last = mm(PQ[0:CROWS, TS[t] + skip:TS[t] + TP], c48[:, t, :], ident[0:TP, skip:TP],
                          start=(t == 0), stop=True, skip_group_check=True)
            last.then_inc(pe_cT, 1)
            yield "load"

            def units(n, u):
                P = PG[:, (2 * n + u) % 3, :]
                if n < SCH:
                    name, first_col, width = "sgu", n * 2 * INNER, INNER
                    need(pe, name)
                else:
                    j = n - SCH
                    name, first_col, width = f"egu{j // 2}", (j % 2) * 256, 128
                    need(pe, name)
                    mm(P[:, N:N + NB], hi[f"sel{j // 6}"][:, j % 6, :], cT[:, u * NB:(u + 1) * NB], start=True, stop=True)
                from_stack(P[0:width, 0:N], stack_e, name, slice(first_col + u * width, first_col + (u + 1) * width)
                           ).then_inc(pe_value if u else pe_gate, 1)

            def expert_down(n):
                w = whole["sd"][:, n, :] if n < SCH else whole["ed"][:, n - SCH, :]
                pe.wait_ge(hid_ready, at(hid_ready, g, n + 1))
                down(PA, hid[0:(INNER if n < SCH else 128), n % 2, :], w, n == 0, n == SCH + ECH - 1).then_inc(pe_down, 1)

            pe.wait_ge(act_moved, at(act_moved, g, 1))
            units(0, 0)
            units(0, 1)
            yield "first"
            pe.wait_ge(whole_in["sd"], 16)
            pe.wait_ge(whole_in["ed"], 16)
            pe.wait_ge(act_cT, at(act_cT, g, 1))
            for n in range(SCH + ECH):
                if n + 1 < SCH + ECH:
                    if n:
                        pe.wait_ge(hid_ready, at(hid_ready, g, n))
                    units(n + 1, 0)
                if n == 1:
                    pe.wait_ge(out_ready, at(out_ready, g, 0))
                if n:
                    expert_down(n - 1)
                if n == 1:
                    need(pe, "sel1")
                    for t in range(TILES):
                        mm(tile_out(PA, t), cT[:, TS[t]:TS[t] + TP], hi["bd"][:, 0, :],
                           start=False, stop=False, skip_group_check=True)
                if n + 1 < SCH + ECH:
                    if n < SCH:
                        pe.wait_ge(act_silu, at(act_silu, g, n + 1))
                    else:
                        pe.wait_ge(gates_done, at(gates_done, g, 2 * (n - SCH) + 2))
                    units(n + 1, 1)
                yield f"e{n}"
            expert_down(SCH + ECH - 1)
            yield "end"

        @block.tensor
        def _(pe):
            pipeline(pe, {"F": pe_front, "M": pe_mid, "Y": pe_experts}, PE_ORDER)


COLUMNS = (("ln_w", 4), ("ln_b", 4), ("decay", 2), ("first", 2), ("egb", ECH), ("eub", ECH), ("sgb", SCH), ("sub", SCH), ("ident", 128))
FRONT_STEPS, MID_STEPS = 52, 75


def _order(*parts):
    entries = (e.split(":") for part in parts for e in part.split())
    return [(track, int(step) if step.isdigit() else step) for track, step in entries]


PE_ORDER = _order(
    "F:tok Y:load Y:first",
    "Y:e0 M:tr2",
    "Y:e1",
    "Y:e2 F:tr1",
    "Y:e3 F:k",
    "Y:e4 F:v F:r",
    "Y:e5 M:rf M:mix0",
    "Y:e6 M:mix1 M:mix2",
    "Y:e7 M:mix3 M:mix4",
    "Y:e8 M:mix5 M:mixed",
    "Y:e9",
    "Y:e10 M:tr3",
    "Y:e11 M:logits",
    "Y:e12 F:o",
    "Y:e13",
)
ACT_ORDER = _order(
    "W:2 F:tok W:4 Y:load Y:e0 M:ln2",
    "Y:e1 M:tr2 F:ln1 W:1",
    "Y:e2 W:2",
    "Y:e3 F:tr1",
    "Y:e4 F:k W:1",
    "Y:e5 F:v F:r W:1",
    "Y:e6 F:exps M:rf M:mix0",
    "Y:e7 M:mix1 M:mix2",
    "Y:e8 M:mix3 M:mix4",
    "Y:e9 M:mix5 F:x0",
    "Y:e10 M:ln3",
    "Y:e11 M:tr3",
    "Y:e12 M:logits",
    "Y:e13",
)
DVE_ORDER = _order(
    "M:ln2 F:8",
    "Y:e0 F:ln1",
    "Y:e1 M:tr2",
    "Y:e2",
    "Y:e3 F:tr1",
    "Y:e4 F:3",
    "Y:e5 F:5",
    "F:3 Y:e6 F:exps",
    "Y:e7 F:6",
    "Y:e8 F:5",
    "Y:e9 F:1 M:ln3",
    "Y:e10 F:5 M:tr3",
    "Y:e11 F:z M:logits",
    "Y:e12 M:10",
    "Y:e13 F:x1 M:routed",
)


def _stack(w):
    import numpy as np
    wt = w.T
    return np.stack([wt[0:128], np.concatenate([wt[128:192]] * 2)], axis=1)


def _by_channel(x):
    import numpy as np
    x = x.reshape(C)
    return np.stack([x[0:128], np.concatenate([x[128:192]] * 2)], axis=1)


def kernel(**inputs):
    import numpy as np
    import concourse.bacc as bacc
    from concourse.bass_utils import run_bass_kernel_spmd

    I = {k: np.asarray(v) for k, v in inputs.items()}
    a = {}
    x = I["x"].reshape(GROUPS, IMGS, SIDE, PATCH, SIDE, PATCH).transpose(0, 3, 5, 1, 2, 4)
    pat = np.zeros((GROUPS, PIX, IMGS, T), np.float32)
    pat[..., 1:] = x.reshape(GROUPS, PIX, IMGS, SIDE * SIDE)
    a["patches"] = pat.reshape(GROUPS, 2, 128, N).transpose(0, 2, 1, 3)
    cls = np.zeros((CLS, C), np.float32)
    cls[0::32] = I["cls_tok"].reshape(1, C)
    a["w_cls"] = cls
    a["w_mask"] = ((np.arange(N) % T == 0) & (np.arange(CLS) % 32 == 0)[:, None]).astype(np.float32)
    p = np.arange(ECH * 128) // INNER
    sel = np.concatenate([(p == np.arange(EXPERTS)[:, None])] * 2 + [np.zeros((CROWS - 2 * EXPERTS, ECH * 128), bool)]).astype(np.float32)
    a["w_sel0"], a["w_sel1"] = sel[:, :ECH * 64], sel[:, ECH * 64:]
    before = (np.arange(EGROUPS)[None, :] < np.arange(EGROUPS)[:, None]).astype(np.float32)
    a["router_rows"] = np.concatenate([I["L0_ffn_router_b"].reshape(-1), I["L0_ffn_corr_bias"].reshape(-1), before.reshape(-1)])[None]
    col = {"ident": np.eye(128, dtype=np.float32)}
    for n in "wb":
        col["ln_" + n] = np.concatenate([_by_channel(I[f"L0_attn_ln{i}_{n}"]) for i in (1, 2)], axis=1)
    for n in ("decay", "first"):
        col[n] = _by_channel(I["L0_attn_" + n])
    col["egb"], col["eub"] = (I["L0_ffn_" + n].reshape(ECH, 128).T for n in ("gbg", "gbu"))
    for name, n in (("sgb", "sbg"), ("sub", "sbu")):
        col[name] = np.concatenate([I["L0_ffn_" + n].reshape(SCH, INNER).T, np.zeros((128 - INNER, SCH), np.float32)])
    a["columns"] = np.concatenate([col[name] for name, _ in COLUMNS], axis=1)
    a["w_tok"] = I["L0_tok_W"].T.reshape(2, 128, C).transpose(1, 0, 2)
    for n in ("k", "v", "r"):
        w = _stack(I[f"L0_attn_W{n}_a"])
        a[f"w_{n}"] = np.concatenate([w, np.zeros_like(w[:, :, 0:64]), w[:, :, 128:]], axis=2)
    a["w_o"] = _stack(I["L0_attn_Wo_a"])
    up = _stack(I["L0_attn_Wk_f"])
    a["w_up0"], a["w_up1"] = up[:, :, :HID // 2], up[:, :, HID // 2:]
    a["w_rf"] = _stack(I["L0_attn_Wr_f"])
    a["w_down"] = I["L0_attn_Wv_f"].T.reshape(UPS, 128, C).transpose(1, 0, 2)
    a["w_router"] = _stack(I["L0_ffn_router_w"])
    sg, su = _stack(I["L0_ffn_sWg"].T), _stack(I["L0_ffn_sWu"].T)
    a["w_sgu"] = np.stack([sg.reshape(128, 2, SCH, INNER), su.reshape(128, 2, SCH, INNER)], axis=3)
    a["w_sd"] = I["L0_ffn_sWd"].reshape(SCH, INNER, C).transpose(1, 0, 2)
    bd, sbd = I["L0_ffn_gbd"], I["L0_ffn_sbd"].reshape(1, C)
    a["w_bd"] = np.concatenate([bd, bd, bd, sbd, np.zeros((15, C), np.float32), sbd])
    eg, eu = (_stack(I["L0_ffn_" + n].transpose(0, 2, 1).reshape(EXPERTS * INNER, C)) for n in ("gWg", "gWu"))
    egu = np.stack([eg.reshape(128, 2, ECH // 2, 2, 128), eu.reshape(128, 2, ECH // 2, 2, 128)], axis=4)
    a["w_ed"] = I["L0_ffn_gWd"].reshape(ECH, 128, C).transpose(1, 0, 2)
    for i in range(ECH // 2):
        a[f"w_egu{i}"] = egu[:, :, i]
    for name, prt, slots, cols, _ in PIECES:
        a[f"w_{name}"] = a[f"w_{name}"].reshape(prt, slots * cols)

    nc = bacc.Bacc("TRN2", target_bir_lowering=False, num_devices=1, dynamic_dma_scratch_size=1024)
    arrays = {f"in_{k}": np.ascontiguousarray(x) for k, x in a.items()}
    A = {k: nc.dram_tensor(f"in_{k}", arrays[f"in_{k}"].shape, F32, kind="ExternalInput").ap() for k in a}
    A["out"] = nc.dram_tensor("out", (GROUPS, N, C), F32, kind="ExternalOutput").ap()
    build(nc, A)
    r = run_bass_kernel_spmd(nc, [arrays], core_ids=[0])
    return r.results[0]["out"].reshape(BATCH, T, C)
```
